# Optimizing a Trainium2 kernel written in Bass

```python
import numpy as np
import jax
import jax.numpy as jnp

def _softmax(x, axis=-1):
    return jax.nn.softmax(x, axis=axis)
def _gelu(x):
    return jax.nn.gelu(x, approximate=True)
def _silu(x):
    return jax.nn.silu(x)
def _sigmoid(x):
    return jax.nn.sigmoid(x)
def _layernorm(x, axis=-1, eps=1e-5):
    m = jnp.mean(x, axis=axis, keepdims=True)
    v = jnp.var(x, axis=axis, keepdims=True)
    return (x - m) / jnp.sqrt(v + eps)
def _scatter_add(tgt, idx, src, axis=0):
    return tgt.at[idx].add(src)
def _segment_sum(src, seg, n):
    return jax.ops.segment_sum(src, seg, n)

kernel_name = 'mk_conv_seq_d1_conv_nchw192_cba063'

def setup_inputs(seed: int = 0):
    np.random.seed(seed)
    _w = jnp.asarray
    def _rec_inputs():
        import jax
        import jax.numpy as jnp
        _gk = jax.random.key(seed)
        x = 7.572e-06 + 1 * jax.random.normal(jax.random.fold_in(_gk, 1), (16, 192, 56, 56), jnp.float32)
        return x
    x = _rec_inputs()
    def _L0_conv_setup():
        import jax, jax.numpy as jnp
        import numpy as np
        DIM = 192
        WIN = 7
        HEADS = 6
        SHIFT = 3
        HID = 4 * DIM

        def _ln(x, w, b, eps=1e-05):
            m = jnp.mean(x, axis=-1, keepdims=True)
            v = jnp.var(x, axis=-1, keepdims=True)
            return (x - m) * jax.lax.rsqrt(v + eps) * w + b
        key = jax.random.key(seed)
        ks = jax.random.split(key, 8)
        B, C, H, W = (16, DIM, 56, 56)
        s = lambda k, shape, fan: jax.random.normal(k, shape, jnp.float32) * (1.0 / np.sqrt(fan))
        return {'x': jax.random.normal(ks[0], (B, C, H, W), jnp.float32), 'norm1_w': jnp.ones((C,), jnp.float32), 'norm1_b': jnp.zeros((C,), jnp.float32), 'qkv_w': s(ks[1], (3 * C, C), C), 'qkv_b': jnp.zeros((3 * C,), jnp.float32), 'proj_w': s(ks[2], (C, C), C), 'proj_b': jnp.zeros((C,), jnp.float32), 'norm2_w': jnp.ones((C,), jnp.float32), 'norm2_b': jnp.zeros((C,), jnp.float32), 'fc1_w': s(ks[3], (HID, C), C), 'fc1_b': jnp.zeros((HID,), jnp.float32), 'fc2_w': s(ks[4], (C, HID), HID), 'fc2_b': jnp.zeros((C,), jnp.float32)}
    _L0_conv_all = _L0_conv_setup()
    _L0_conv_in = {k: v for k, v in _L0_conv_all.items() if k in ('norm1_w', 'norm1_b', 'qkv_w', 'qkv_b', 'proj_w', 'proj_b', 'norm2_w', 'norm2_b', 'fc1_w', 'fc1_b', 'fc2_w', 'fc2_b', )}
    del _L0_conv_all

    return {
        "x": x,
        "L0_conv_norm1_w": _L0_conv_in["norm1_w"],
        "L0_conv_norm1_b": _L0_conv_in["norm1_b"],
        "L0_conv_qkv_w": _L0_conv_in["qkv_w"],
        "L0_conv_qkv_b": _L0_conv_in["qkv_b"],
        "L0_conv_proj_w": _L0_conv_in["proj_w"],
        "L0_conv_proj_b": _L0_conv_in["proj_b"],
        "L0_conv_norm2_w": _L0_conv_in["norm2_w"],
        "L0_conv_norm2_b": _L0_conv_in["norm2_b"],
        "L0_conv_fc1_w": _L0_conv_in["fc1_w"],
        "L0_conv_fc1_b": _L0_conv_in["fc1_b"],
        "L0_conv_fc2_w": _L0_conv_in["fc2_w"],
        "L0_conv_fc2_b": _L0_conv_in["fc2_b"],
    }

def reference(x, L0_conv_norm1_w, L0_conv_norm1_b, L0_conv_qkv_w, L0_conv_qkv_b, L0_conv_proj_w, L0_conv_proj_b, L0_conv_norm2_w, L0_conv_norm2_b, L0_conv_fc1_w, L0_conv_fc1_b, L0_conv_fc2_w, L0_conv_fc2_b):
    import jax
    import jax.numpy as jnp
    def _L0_conv_ref(x, norm1_w, norm1_b, qkv_w, qkv_b, proj_w, proj_b, norm2_w, norm2_b, fc1_w, fc1_b, fc2_w, fc2_b):
        import jax, jax.numpy as jnp
        import numpy as np
        DIM = 192
        WIN = 7
        HEADS = 6
        SHIFT = 3
        HID = 4 * DIM

        def _ln(x, w, b, eps=1e-05):
            m = jnp.mean(x, axis=-1, keepdims=True)
            v = jnp.var(x, axis=-1, keepdims=True)
            return (x - m) * jax.lax.rsqrt(v + eps) * w + b
        B, C, H, W = x.shape
        shift = SHIFT if H > WIN and W > WIN else 0
        shortcut = x
        xl = jnp.transpose(x, (0, 2, 3, 1))
        xl = _ln(xl, norm1_w, norm1_b)
        if shift > 0:
            xl = jnp.roll(xl, shift=(-shift, -shift), axis=(1, 2))
        nH, nW = (H // WIN, W // WIN)
        xw = xl.reshape(B, nH, WIN, nW, WIN, C)
        xw = jnp.transpose(xw, (0, 1, 3, 2, 4, 5)).reshape(-1, WIN * WIN, C)
        Bw, N, _ = xw.shape
        dh = C // HEADS
        qkv = jnp.einsum('bnc,oc->bno', xw, qkv_w) + qkv_b
        qkv = qkv.reshape(Bw, N, 3, HEADS, dh)
        q, k, v = (qkv[:, :, 0], qkv[:, :, 1], qkv[:, :, 2])
        scale = dh ** (-0.5)
        attn = jnp.einsum('bnhd,bmhd->bhnm', q, k) * scale
        attn = jax.nn.softmax(attn, axis=-1)
        out = jnp.einsum('bhnm,bmhd->bnhd', attn, v).reshape(Bw, N, C)
        out = jnp.einsum('bnc,oc->bno', out, proj_w) + proj_b
        xl = out.reshape(B, nH, nW, WIN, WIN, C)
        xl = jnp.transpose(xl, (0, 1, 3, 2, 4, 5)).reshape(B, H, W, C)
        if shift > 0:
            xl = jnp.roll(xl, shift=(shift, shift), axis=(1, 2))
        xl = _ln(xl, norm2_w, norm2_b)
        h = jnp.einsum('bhwc,oc->bhwo', xl, fc1_w) + fc1_b
        h = jax.nn.gelu(h, approximate=False)
        h = jnp.einsum('bhwo,co->bhwc', h, fc2_w) + fc2_b
        return jnp.transpose(h, (0, 3, 1, 2)) + shortcut

    def _gn(v, G=32, eps=1e-5):
        B_, C_, H_, W_ = v.shape
        g = v.reshape(B_, G, C_ // G, H_, W_)
        m = jnp.mean(g, axis=(2, 3, 4), keepdims=True)
        s = jnp.var(g, axis=(2, 3, 4), keepdims=True)
        return ((g - m) / jnp.sqrt(s + eps)).reshape(v.shape)

    def _ln_c(v, eps=1e-6):
        m = jnp.mean(v, axis=1, keepdims=True)
        s = jnp.var(v, axis=1, keepdims=True)
        return (v - m) / jnp.sqrt(s + eps)

    def _ln_t(v, eps=1e-5):
        m = jnp.mean(v, axis=-1, keepdims=True)
        s = jnp.var(v, axis=-1, keepdims=True)
        return (v - m) / jnp.sqrt(s + eps)

    def _to_tokens(v):
        B_, C_, H_, W_ = v.shape
        return v.reshape(B_, C_, H_ * W_).transpose(0, 2, 1)
    def _from_tokens(t, like):
        B_, C_, H_, W_ = like.shape
        return t.transpose(0, 2, 1).reshape(B_, C_, H_, W_)

    x = _L0_conv_ref(x, L0_conv_norm1_w, L0_conv_norm1_b, L0_conv_qkv_w, L0_conv_qkv_b, L0_conv_proj_w, L0_conv_proj_b, L0_conv_norm2_w, L0_conv_norm2_b, L0_conv_fc1_w, L0_conv_fc1_b, L0_conv_fc2_w, L0_conv_fc2_b)
    return x


_drawn_inputs = setup_inputs


def setup_inputs(seed=0):
    import zlib

    import numpy as np

    out = dict(_drawn_inputs(seed))
    spreads = {'L0_conv_norm1_w': (1.0, 0.2),
     'L0_conv_norm1_b': (0.0, 0.1),
     'L0_conv_qkv_b': (0.0, 0.1),
     'L0_conv_proj_b': (0.0, 0.1),
     'L0_conv_norm2_w': (1.0, 0.2),
     'L0_conv_norm2_b': (0.0, 0.1),
     'L0_conv_fc1_b': (0.0, 0.1),
     'L0_conv_fc2_b': (0.0, 0.1)}
    factors = {}
    for name, (base, spread) in spreads.items():
        noise = np.random.default_rng([zlib.crc32(name.encode()), seed]).standard_normal(out[name].shape)
        drawn = base * np.exp(spread * noise) if base else spread * noise
        out[name] = jnp.asarray(drawn.astype(out[name].dtype))
    for name, factor in factors.items():
        out[name] = (out[name] * factor).astype(out[name].dtype)
    return out
```

```python
import numpy as np
import concourse.bass as bass
from concourse import mybir
from contextlib import ExitStack

F32 = mybir.dt.float32
F32R = mybir.dt.float32r
ALU = mybir.AluOpType
ACT = mybir.ActivationFunctionType
AX = mybir.AxisListType

B, C, H, W = 16, 192, 56, 56
WIN, SHIFT, HEADS = 7, 3, 6
DH = C // HEADS
HID = 4 * C
N = WIN * WIN
NW = W // WIN
T = NW * N
UPB = H // WIN
UNITS = B * UPB
CM = 128
CR = C - CM
MT = HID // 128
PAIRS = NW // 2
TP = 2 * N
WP = 64
SP = WP + N
ROWS = [2, 2, 2, 1]
CHUNKS = [[W * r for r in ROWS], [TP] * PAIRS]
TM = max(CHUNKS[0])
SLOTS = 4
SCALE = float(DH) ** -0.5
EPS = 1e-5

PA = 4 * W - SHIFT
PB = T - SHIFT
SMALL = 16 * (12 + 6 + 4 + MT)
LOADS = 6

BANK_USES = [("ln1", 0, 0), ("ln1", 1, 1), ("xn1", 0, 2), ("xn1", 1, 3),
             ("qkv", 0, 0), ("qkv", 1, 1), ("qkv", 2, 2), ("qkv", 3, 3), ("qkv", 4, 0),
             ("vt", 0, 1), ("vt", 1, 2),
             ("s", 0, 0), ("s", 1, 1), ("s", 2, 2), ("s", 3, 3),
             ("pt", 0, 3), ("pt", 1, 0), ("o", 0, 1), ("o", 1, 2), ("pt", 2, 3), ("pt", 3, 0),
             ("proj", 0, 3), ("proj", 1, 0), ("ln2", 0, 1), ("ln2", 1, 2), ("xn2", 0, 0), ("xn2", 1, 3)]
BANK_OF = {(n, i): b for n, i, b in BANK_USES}
USES = [sum(1 for u in BANK_USES if u[2] == b) for b in range(4)]
USE_NO = {(n, i): sum(1 for u in BANK_USES[:k] if u[2] == b) for k, (n, i, b) in enumerate(BANK_USES)}

PARTS = [((4, 6), (0, 4)), ((0, 4), (0, 2)), ((0, 4), (2, 4))]

QKV_COLS = [(2 * C, CM), (2 * C + CM, CR), (0, CM), (C, CM), (CM, CR), (C + CM, CR)]
QKV_TILES = [(0, 128), (128, 64), (192, 128), (320, 128), (448, 128)]


def nth(unit, per_unit, i):
    return unit * per_unit + (i + 1)


def swin_block_program(nc, x, n1w, n1b, qkv_wt, qkv_b, proj_wt, proj_b, n2w, n2b,
                       fc1_wt, fc1_b, fc2_wt, fc2_b, out):
    ctx = ExitStack()
    with ctx:
        def sb(name, shape, dt=F32):
            return ctx.enter_context(nc.sbuf_tensor(name, shape, dt))

        def sem(name):
            return ctx.enter_context(nc.semaphore(name))

        ident = sb("ident", [128, 128])
        half = sb("half", [128, PAIRS])
        eps = sb("eps", [128, PAIRS])
        NQ, NF = 3 * C, HID
        wq = [sb(f"wq_{p}", [128, NQ], F32R) for p in ("mh", "ml", "rh", "rl")]
        wp = [sb(f"wp_{p}", [128, C], F32R) for p in ("mh", "ml", "rh", "rl")]
        w1 = [sb(f"w1_{p}", [128, NF], F32R) for p in ("mh", "ml", "rh", "rl")]
        w2h = sb("w2h", [128, MT, C], F32R)
        w2l = sb("w2l", [128, MT, CM], F32R)
        w2r = sb("w2r", [128, MT, 128], F32R)
        bq = sb("bq", [128, 5])
        bp = sb("bp", [128, 2])
        b1 = sb("b1", [128, MT])
        b2 = sb("b2", [128, 2])
        raw_m = sb("raw_m", [128, NF])
        raw_r = sb("raw_r", [128, NF])
        raw_2 = sb("raw_2", [128, MT, C])
        scl_m = sb("scl_m", [128, NF])
        scl_r = sb("scl_r", [128, NF])
        nwb = sb("nwb", [128, 8])

        xt = sb("xt", [128, SLOTS, 2, T])
        st = [sb(f"st{i}", [TM, PAIRS, 6]) for i in range(2)]
        mv = [sb(f"mv{i}", [TM, PAIRS, 2]) for i in range(2)]
        ve = [sb(f"ve{i}", [TM, PAIRS]) for i in range(2)]
        rs = [sb(f"rs{i}", [TM, PAIRS]) for i in range(2)]
        xn = sb("xn", [TM, PAIRS, C])
        x1 = [sb(f"x1_{p}", [128, T], F32R) for p in ("h", "l", "r")]
        x2 = [sb(f"x2_{p}", [128, T], F32R) for p in ("h", "l", "r")]
        qm = sb("qm", [128, T])
        km = sb("km", [128, T])
        qr = sb("qr", [CR, T])
        kr = sb("kr", [CR, T])
        vm = sb("vm", [128, NW, WP])
        vr = sb("vr", [CR, NW, WP])
        vbd = sb("vbd", [128, NW, 3, WP])
        pr = sb("pr", [SP, PAIRS, HEADS * WP])
        mx = sb("mx", [SP, HEADS, PAIRS])
        sm = sb("sm", [SP, HEADS, PAIRS])
        rc = sb("rc", [SP, HEADS, PAIRS])
        pt = sb("pt", [SP, 2, 3, 128])
        o = [sb(f"o_{p}", [128, T], F32R) for p in ("h", "l", "r")]
        pj = sb("pj", [128, 2, T])
        hf = sb("hf", [128, 2, T])
        hh = sb("hh", [128, 2, T], F32R)
        hl = sb("hl", [128, 2, T], F32R)
        yl = sb("yl", [CR, T])
        xr = sb("xr", [CR, T])

        att = ctx.enter_context(nc.psum_tensor("att", [128, 4, 512], F32))
        hid = [ctx.enter_context(nc.psum_tensor(f"hid{i}", [128, 512], F32)) for i in range(2)]
        yps = [ctx.enter_context(nc.psum_tensor(f"yps{i}", [128, 512], F32)) for i in range(2)]

        def bank(name, i):
            return att[:, BANK_OF[name, i], :]

        s_raw = [sem(f"raw_loaded_{i}") for i in range(4)]
        s_small = sem("small_loaded")
        s_id = sem("ident_made")
        s_zero = sem("pads_zeroed")
        s_scaled = sem("weights_scaled")
        s_split = sem("weights_split")
        s_rawfree = sem("raw_used_by_bias_products")
        s_bias_mm = sem("bias_products_done")
        s_bias = sem("biases_ready")
        s_x = [sem(f"x_loaded_{i}") for i in range(SLOTS)]
        s_st = [sem(f"out_stored_{i}") for i in range(SLOTS)]
        s_bank = [sem(f"att_bank_free_{i}") for i in range(4)]
        s_pe = {n: sem(f"pe_{n}") for n in ("ln1", "xn1", "qkv", "vt", "s", "pt", "o", "proj", "ln2", "xn2", "fc1", "fc2")}
        s_stats = [sem(f"bn_stats_done_{i}") for i in range(2)]
        s_seen = sem("bn_stats_seen")
        s_mv = [sem(f"mean_var_done_{i}") for i in range(2)]
        s_ve = [sem(f"var_eps_done_{i}") for i in range(2)]
        s_rs = [sem(f"rstd_done_{i}") for i in range(2)]
        s_norm = [sem(f"normalised_{i}") for i in range(2)]
        s_hi = {n: sem(f"hi_{n}") for n in ("x1", "x2", "o")}
        s_lo = {n: sem(f"lo_{n}") for n in ("x1", "x2", "o")}
        s_qkv = sem("qkv_in_sbuf")
        s_vbd = sem("vbd_ready")
        s_mx = sem("row_max")
        s_sub = sem("max_subtracted")
        s_exp = sem("exp_done")
        s_sum = sem("row_sum")
        s_rec = sem("sum_reciprocal")
        s_prob = sem("probabilities")
        s_ptc = sem("pt_in_sbuf")
        s_pj = sem("proj_in_sbuf")
        s_gelu = sem("gelu_done")
        s_hh = sem("hidden_hi")
        s_hl = sem("hidden_lo")
        s_ylo = sem("y_rem_lo_copied")
        s_xr = sem("y_rem_residual")
        s_fin = sem("output_ready")

        xf = x.rearrange("b c h w -> b c (h w)")
        of = out.rearrange("b c h w -> b c (h w)")

        def runs(i):
            a = i * T + SHIFT * W + SHIFT
            b = (a + PA) % (H * W)
            return [(a, PA, 0), (b, PB - PA, PA), (a - SHIFT, SHIFT, PB)]

        def rows_by_window(ap, j):
            r0, n = sum(ROWS[:j]), ROWS[j]
            return ap.rearrange("p (w r c) -> p r w c", r=WIN, w=NW)[:, r0:r0 + n]

        def windows_by_row(ap, j):
            return ap.rearrange("p (r w c) -> p w r c", r=WIN, w=NW)[:, 2 * j:2 * j + 2]

        def probs(i):
            (h0, h1), (j0, j1) = PARTS[i]
            return pr.rearrange("p j (h m) -> p h j m", h=HEADS)[:, h0:h1, j0:j1, 0:N]

        def rows(t, i):
            (h0, h1), (j0, j1) = PARTS[i]
            return t[:, h0:h1, j0:j1]

        def five(ps, w, c0, m, act, n=T):
            wmh, wml, wrh, wrl = w
            xh, xl, xrr = act
            nc.tensor.matmul(ps, wmh[:, c0:c0 + m], xh[:, :], start=True, stop=False)
            nc.tensor.matmul(ps, wml[:, c0:c0 + m], xh[:, :], start=False, stop=False)
            nc.tensor.matmul(ps, wmh[:, c0:c0 + m], xl[:, :], start=False, stop=False)
            nc.tensor.matmul(ps, wrh[:, c0:c0 + m], xrr[:, :], start=False, stop=False)
            return nc.tensor.matmul(ps, wrl[:, c0:c0 + m], xrr[:, :], start=False, stop=True)

        block = ctx.enter_context(nc.Block())

        @block.sync
        def _(sp):
            def load(b, i):
                u = b * UPB + i
                slot = i % SLOTS
                if not (isinstance(u, int) and u < SLOTS):
                    sp.wait_ge(s_st[slot], (b * 2 + i // SLOTS) * (16 * LOADS))
                for px, n, at in runs(i):
                    sp.dma_start(xt[:, slot, 0, at:at + n], xf[b, 0:CM, px:px + n]).then_inc(s_x[slot], 16)
                    sp.dma_start(xt[0:CR, slot, 1, at:at + n], xf[b, CM:C, px:px + n]).then_inc(s_x[slot], 16)

            def store(b, i):
                slot = i % SLOTS
                sp.wait_ge(s_fin, b * (2 * UPB) + (2 * i + 2))
                for px, n, at in runs(i):
                    sp.dma_start(of[b, 0:CM, px:px + n], xt[:, slot, 0, at:at + n]).then_inc(s_st[slot], 16)
                    sp.dma_start(of[b, CM:C, px:px + n], xt[0:CR, slot, 1, at:at + n]).then_inc(s_st[slot], 16)

            for k, (vec, cols) in enumerate(((n1w, 0), (n1b, 2), (n2w, 4), (n2b, 6))):
                sp.dma_start(nwb[:, cols:cols + 1], vec[0:CM].rearrange("(p a) -> p a", a=1)).then_inc(s_small, 16)
                for h in range(2):
                    sp.dma_start(nwb[h * CR:(h + 1) * CR, cols + 1:cols + 2],
                                 vec[CM:C].rearrange("(p a) -> p a", a=1)).then_inc(s_small, 16)
            at = 0
            for c0, m in QKV_COLS:
                t, r = next((k, at - s) for k, (s, n) in enumerate(QKV_TILES) if s <= at < s + n)
                sp.dma_start(bq[r:r + m, t:t + 1], qkv_b[c0:c0 + m].rearrange("(p a) -> p a", a=1)).then_inc(s_small, 16)
                at += m
            for vec, dst in ((proj_b, bp), (fc2_b, b2)):
                sp.dma_start(dst[:, 0:1], vec[0:CM].rearrange("(p a) -> p a", a=1)).then_inc(s_small, 16)
                sp.dma_start(dst[0:CR, 1:2], vec[CM:C].rearrange("(p a) -> p a", a=1)).then_inc(s_small, 16)
            for m in range(MT):
                sp.dma_start(b1[:, m:m + 1], fc1_b[m * 128:(m + 1) * 128].rearrange("(p a) -> p a", a=1)).then_inc(s_small, 16)
            at = 0
            for c0, m in QKV_COLS:
                sp.dma_start(raw_m[:, at:at + m], qkv_wt[0:CM, c0:c0 + m]).then_inc(s_raw[0], 16)
                for h in range(2):
                    sp.dma_start(raw_r[h * CR:(h + 1) * CR, at:at + m], qkv_wt[CM:C, c0:c0 + m]).then_inc(s_raw[0], 16)
                at += m
            load(0, 0)
            load(0, 1)
            sp.dma_start(raw_2[:, :, :], fc2_wt.rearrange("(m p) n -> p m n", p=128)).then_inc(s_raw[3], 16)
            for n, (wt, cols) in enumerate(((proj_wt, C), (fc1_wt, NF))):
                sp.wait_ge(s_rawfree, n + 1)
                sp.dma_start(raw_m[:, 0:cols], wt[0:CM, :]).then_inc(s_raw[n + 1], 16)
                for h in range(2):
                    sp.dma_start(raw_r[h * CR:(h + 1) * CR, 0:cols], wt[CM:C, :]).then_inc(s_raw[n + 1], 16)

            def step(b, i):
                if i < UPB - 1:
                    load(b, i + 1)
                elif not (isinstance(b, int) and b == B - 1):
                    load(b + 1, 0)
                if i > 0:
                    store(b, i - 1)
                elif not (isinstance(b, int) and b == 0):
                    store(b - 1, UPB - 1)

            for i in range(1, UPB):
                step(0, i)
            with sp.Fori(1, B - 1) as b:
                for i in range(UPB):
                    step(b, i)
            for i in range(UPB):
                step(B - 1, i)
            store(B - 1, UPB - 1)
            for slot in range(SLOTS):
                sp.wait_ge(s_st[slot], 16 * LOADS * (UNITS // SLOTS))

        def steps(eng, attention_and_mlp, last_mlp):
            for k in range(SLOTS):
                attention_and_mlp(k, k, 0)
            with eng.Fori(1, UNITS // SLOTS) as it:
                for k in range(SLOTS):
                    attention_and_mlp(it * SLOTS + k, k, it)
            last_mlp(UNITS - 1, SLOTS - 1)

        @block.tensor
        def _(pe):
            pe.wait_ge(s_id, 2)
            pe.wait_ge(s_small, SMALL)

            def claim(name, i, s):
                b = BANK_OF[name, i]
                n = USE_NO[name, i]
                if not isinstance(s, int) or s * USES[b] + n > 0:
                    pe.wait_ge(s_bank[b], s * USES[b] + n)

            pe.wait_ge(s_raw[0], 16 * 18)
            for t, (c0, m) in enumerate(QKV_TILES):
                nc.tensor.matmul(hid[0][0:m, t:t + 1], raw_m[:, c0:c0 + m], nwb[:, 2:3], start=True, stop=False)
                last = nc.tensor.matmul(hid[0][0:m, t:t + 1], raw_r[0:CR, c0:c0 + m], nwb[0:CR, 3:4], start=False, stop=True)
            last.then_inc(s_bias_mm, 1)
            pe.wait_ge(s_raw[2], 16 * 3)
            for m in range(MT):
                nc.tensor.matmul(hid[1][:, m:m + 1], raw_m[:, m * 128:(m + 1) * 128], nwb[:, 6:7], start=True, stop=False)
                last = nc.tensor.matmul(hid[1][:, m:m + 1], raw_r[0:CR, m * 128:(m + 1) * 128], nwb[0:CR, 7:8], start=False, stop=True)
            last.then_inc(s_bias_mm, 1)
            pe.wait_ge(s_zero, 1)
            pe.wait_ge(s_split, 4)
            pe.wait_ge(s_bias, 2)

            def to_tokens(name, ln, s, tile_m, tile_r):
                for j, n in enumerate(CHUNKS[ln]):
                    c, cc = j // 2, j % 2
                    if cc == 0:
                        claim(name, c, s)
                    at = sum(CHUNKS[ln][:j])
                    ps = bank(name, c)[0:n, cc * C:(cc + 1) * C]
                    nc.tensor.transpose(ps[:, 0:CM], tile_m[:, at:at + n], ident[:, :])
                    last = nc.tensor.transpose(ps[:, CM:C], tile_r[:, at:at + n], ident[0:CR, 0:CR])
                    if cc == 1:
                        last.then_inc(s_pe[name], 1)

            def to_channels(name, ln, s, place):
                claim(name, 0, s)
                claim(name, 1, s)
                for g, (c0, m) in enumerate(((0, CM), (CM, CR))):
                    for j, n in enumerate(CHUNKS[ln]):
                        if g == 0 and j < 3:
                            pe.wait_ge(s_norm[ln], nth(s, PAIRS, j + (j == 2)))
                        last = nc.tensor.transpose(place(bank(name, g)[0:m, 0:T], j), xn[0:n, j, c0:c0 + m], ident[0:n, 0:n])
                    last.then_inc(s_pe[name], 1)

            def fc1(v, m):
                if m == 0:
                    pe.wait_ge(s_lo["x2"], nth(v, 2, 1))
                if not isinstance(v, int) or MT * v + m >= 2:
                    pe.wait_ge(s_gelu, v * MT + (m - 1))
                five(hid[m % 2][:, 0:T], w1, m * 128, 128, x2).then_inc(s_pe["fc1"], 1)

            def fc2(v, m):
                pe.wait_ge(s_hl, nth(v, MT, m))
                if m == 0 and not (isinstance(v, int) and v == 0):
                    pe.wait_ge(s_fin, v * 2)
                a, z = m == 0, m == MT - 1
                b = m % 2
                ym, yr = yps[0][:, 0:T], yps[1][:, 0:T]
                nc.tensor.matmul(ym, w2h[:, m, 0:CM], hh[:, b, :], start=a, stop=False)
                nc.tensor.matmul(ym, w2l[:, m, :], hh[:, b, :], start=False, stop=False)
                nc.tensor.matmul(yr, w2r[:, m, :], hh[:, b, :], start=a, stop=z, skip_group_check=True)
                nc.tensor.matmul(ym, w2h[:, m, 0:CM], hl[:, b, :], start=False, stop=z)
                nc.tensor.matmul(yr[0:CR], w2h[:, m, CM:C], hl[:, b, :], start=False, stop=z,
                                 skip_group_check=True).then_inc(s_pe["fc2"], 1)

            def scores(s):
                for g in range(4):
                    claim("s", g, s)
                for w in range(NW):
                    j, wi = w // 2, w % 2
                    for h in range(HEADS):
                        q, k, g, at = (qm, km, h, N * j) if h < 4 else (qr, kr, h - 4, N * (PAIRS + j))
                        last = nc.tensor.matmul(att[WP * wi:WP * wi + N, g, at:at + N],
                                                q[DH * g:DH * g + DH, N * w:N * w + N],
                                                k[DH * g:DH * g + DH, N * w:N * w + N], start=True, stop=True)
                last.then_inc(s_pe["s"], 1)

            def probs_t(s, j):
                claim("pt", j, s)
                pe.wait_ge(s_prob, nth(s, 3, 1 + j // 2))
                for p in range(3):
                    last = nc.tensor.transpose(bank("pt", j)[0:SP, 128 * p:128 * p + SP],
                                               pr[:, j, 2 * WP * p:2 * WP * p + SP], ident[0:SP, 0:SP])
                last.then_inc(s_pe["pt"], 1)

            def weighted(s, j):
                if j == 0:
                    claim("o", 0, s)
                    claim("o", 1, s)
                pe.wait_ge(s_ptc, nth(s, PAIRS, j))
                for wi in range(2):
                    w = 2 * j + wi
                    for p in range(3):
                        ps = bank("o", p // 2)[WP * (p % 2):WP * (p % 2) + WP, N * w:N * w + N]
                        last = nc.tensor.matmul(ps, vbd[0:SP, w, p, :], pt[:, j % 2, p, WP * wi:WP * wi + N],
                                                start=True, stop=True)
                if j == PAIRS - 1:
                    last.then_inc(s_pe["o"], 1)

            def attention_and_mlp(s, k, it):
                v = s - 1
                mlp = not (isinstance(s, int) and s == 0)
                pe.wait_ge(s_x[k], (it + 1) * (16 * LOADS))
                to_tokens("ln1", 0, s, xt[:, k, 0, :], xt[0:CR, k, 1, :])
                if mlp:
                    fc1(v, 0)
                    fc1(v, 1)
                    fc2(v, 0)
                    fc1(v, 2)
                to_channels("xn1", 0, s, rows_by_window)
                if mlp:
                    fc2(v, 1)
                pe.wait_ge(s_lo["x1"], nth(s, 2, 1))
                for t, (c0, m) in enumerate(QKV_TILES):
                    claim("qkv", t, s)
                    five(bank("qkv", t)[0:m, 0:T], wq, c0, m, x1).then_inc(s_pe["qkv"], 1)
                pe.wait_ge(s_qkv, nth(s, 6, 1))
                for j in range(PAIRS):
                    c, cc = j // 2, j % 2
                    if cc == 0:
                        claim("vt", c, s)
                    ps = bank("vt", c)[:, cc * C:(cc + 1) * C]
                    for src, m, c0 in ((vm, CM, 0), (vr, CR, CM)):
                        pair = src[0:m, 2 * j:2 * j + 2, :].rearrange("p w n -> p (w n)")
                        last = nc.tensor.transpose(ps[:, c0:c0 + m], pair, ident[0:m, 0:m])
                    if cc == 1:
                        last.then_inc(s_pe["vt"], 1)
                pe.wait_ge(s_qkv, nth(s, 6, 5))
                scores(s)
                if mlp:
                    fc1(v, 3)
                    fc2(v, 2)
                    fc1(v, 4)
                probs_t(s, 0)
                probs_t(s, 1)
                pe.wait_ge(s_vbd, nth(s, 2, 1))
                weighted(s, 0)
                probs_t(s, 2)
                weighted(s, 1)
                probs_t(s, 3)
                weighted(s, 2)
                weighted(s, 3)
                if mlp:
                    fc2(v, 3)
                pe.wait_ge(s_lo["o"], nth(s, 2, 1))
                for t, (c0, m) in enumerate(((0, CM), (CM, CR))):
                    claim("proj", t, s)
                    five(bank("proj", t)[0:m, 0:T], wp, c0, m, o).then_inc(s_pe["proj"], 1)
                if mlp:
                    fc1(v, 5)
                pe.wait_ge(s_pj, nth(s, 2, 1))
                to_tokens("ln2", 1, s, pj[:, 0, :], pj[0:CR, 1, :])
                if mlp:
                    fc2(v, 4)
                    fc2(v, 5)
                to_channels("xn2", 1, s, windows_by_row)

            def last_mlp(v, k):
                fc1(v, 0)
                fc1(v, 1)
                for m in range(MT):
                    fc2(v, m)
                    if m + 2 < MT:
                        fc1(v, m + 2)

            steps(pe, attention_and_mlp, last_mlp)

        @block.scalar
        def _(act):
            act.wait_ge(s_zero, 1)
            act.wait_ge(s_bias, 2)

            def copy(dst, src, done):
                nc.scalar.activation(dst, src, ACT.Copy).then_inc(done, 1)

            def biased(dst, src, bias, done):
                return nc.scalar.activation(dst, src, ACT.Identity, bias=bias).then_inc(done, 1)

            def hi_parts(name, psname, dst, s, per, first):
                act.wait_ge(s_pe[psname], first)
                copy(dst[0][:, :], bank(psname, 0)[:, 0:T], s_hi[name])
                act.wait_ge(s_pe[psname], first + (per - 1))
                copy(dst[2][0:CR, :], bank(psname, 1)[0:CR, 0:T], s_hi[name])

            def gelu(v, m):
                act.wait_ge(s_pe["fc1"], nth(v, MT, m))
                if not isinstance(v, int) or MT * v + m >= 2:
                    act.wait_ge(s_hl, v * MT + (m - 1))
                nc.scalar.activation(hf[:, m % 2, :], hid[m % 2][:, 0:T], ACT.Gelu, bias=b1[:, m:m + 1]).then_inc(s_gelu, 1)

            def y_low(v):
                act.wait_ge(s_pe["fc2"], nth(v, MT, MT - 1))
                copy(yl[:, :], yps[1][CR:128, 0:T], s_ylo)

            def attention_and_mlp(s, k, it):
                v = s - 1
                mlp = not (isinstance(s, int) and s == 0)
                if mlp:
                    for m in range(3):
                        gelu(v, m)
                hi_parts("x1", "xn1", x1, s, 2, nth(s, 2, 0))
                outs = [[(vm[:, :, 0:N], 0, CM)], [(vr[:, :, 0:N], 0, CR)], [(qm[:, :], 0, CM)],
                        [(km[:, :], 0, CM)], [(qr[:, :], 0, CR), (kr[:, :], CR, CR)]]
                for t, parts in enumerate(outs):
                    act.wait_ge(s_pe["qkv"], nth(s, 5, t))
                    for dst, r, m in parts:
                        src = bank("qkv", t)[r:r + m, 0:T]
                        if t < 2:
                            src = src.rearrange("p (w n) -> p w n", w=NW)
                        last = biased(dst, src, bq[r:r + m, t:t + 1], s_qkv)
                    act.wait_ge(s_qkv, nth(s, 6, t + (t == 4)))
                    act.sem_inc(s_bank[BANK_OF["qkv", t]], 1)
                for i in range(3):
                    act.wait_ge(s_sub, nth(s, 3, i))
                    p = probs(i)
                    nc.scalar.activation(p, p, ACT.Exp, scale=SCALE).then_inc(s_exp, 1)
                if mlp:
                    gelu(v, 3)
                    gelu(v, 4)
                for j in range(PAIRS):
                    act.wait_ge(s_pe["pt"], nth(s, PAIRS, j))
                    src = bank("pt", j)[0:SP, 0:384].rearrange("p (a m) -> p a m", a=3)[:, :, 0:SP]
                    copy(pt[:, j % 2, :, 0:SP], src, s_ptc)
                    act.wait_ge(s_ptc, nth(s, PAIRS, j))
                    act.sem_inc(s_bank[BANK_OF["pt", j]], 1)
                act.wait_ge(s_pe["o"], nth(s, 1, 0))
                copy(o[0][:, :], bank("o", 0)[:, 0:T], s_hi["o"])
                copy(o[2][0:CR, :], bank("o", 1)[0:CR, 0:T], s_hi["o"])
                for t, m in enumerate((CM, CR)):
                    act.wait_ge(s_pe["proj"], nth(s, 2, t))
                    biased(pj[0:m, t, :], bank("proj", t)[0:m, 0:T], bp[0:m, t:t + 1], s_pj)
                    act.wait_ge(s_pj, nth(s, 2, t))
                    act.sem_inc(s_bank[BANK_OF["proj", t]], 1)
                if mlp:
                    gelu(v, 5)
                    y_low(v)
                hi_parts("x2", "xn2", x2, s, 2, nth(s, 2, 0))

            def last_mlp(v, k):
                for m in range(MT):
                    gelu(v, m)
                y_low(v)

            steps(act, attention_and_mlp, last_mlp)

        @block.vector
        def _(dve):
            for t in (vm, vr, vbd, pr, pt, mv[0], mv[1]):
                nc.vector.memset(t[:], 0.0)
            nc.vector.memset(att[:, :, :], 0.0).then_inc(s_zero, 1)

            scaled = split = 0
            dve.wait_ge(s_small, SMALL)
            for n, (w, cols, nw) in enumerate(((wq, NQ, 0), (wp, C, None), (w1, NF, 4))):
                dve.wait_ge(s_raw[n], 16 * (18 if n == 0 else 3))
                sm_, sr_ = raw_m, raw_r
                if nw is not None:
                    if n:
                        dve.wait_ge(s_split, n)
                    nc.vector.tensor_scalar(scl_m[:, 0:cols], raw_m[:, 0:cols], nwb[:, nw:nw + 1], None, ALU.mult).then_inc(s_scaled, 1)
                    nc.vector.tensor_scalar(scl_r[:, 0:cols], raw_r[:, 0:cols], nwb[:, nw + 1:nw + 2], None, ALU.mult).then_inc(s_scaled, 1)
                    scaled += 2
                    dve.wait_ge(s_scaled, scaled)
                    sm_, sr_ = scl_m, scl_r
                nc.vector.tensor_copy(w[0][:, :], sm_[:, 0:cols]).then_inc(s_scaled, 1)
                nc.vector.tensor_copy(w[2][:, :], sr_[:, 0:cols]).then_inc(s_scaled, 1)
                scaled += 2
                dve.wait_ge(s_scaled, scaled)
                nc.vector.tensor_tensor(w[1][:, :], sm_[:, 0:cols], w[0][:, :].bitcast(F32), ALU.subtract)
                nc.vector.tensor_tensor(w[3][:, :], sr_[:, 0:cols], w[2][:, :].bitcast(F32), ALU.subtract).then_inc(s_split, 1)
                if n < 2:
                    if n == 0:
                        dve.wait_ge(s_bias_mm, 1)
                    dve.wait_ge(s_split, n + 1)
                    dve.sem_inc(s_rawfree, 1)
            dve.wait_ge(s_raw[3], 16)
            nc.vector.tensor_copy(w2h[:, :, :], raw_2[:, :, :]).then_inc(s_scaled, 1)
            nc.vector.tensor_copy(w2r[:, :, 0:CR], raw_2[:, :, CM:C]).then_inc(s_scaled, 1)
            dve.wait_ge(s_scaled, scaled + 2)
            nc.vector.tensor_tensor(w2l[:, :, :], raw_2[:, :, 0:CM], w2h[:, :, 0:CM].bitcast(F32), ALU.subtract)
            nc.vector.tensor_tensor(w2r[:, :, CR:128], raw_2[:, :, CM:C], w2r[:, :, 0:CR].bitcast(F32), ALU.subtract).then_inc(s_split, 1)
            dve.wait_ge(s_bias_mm, 1)
            for t, (c0, m) in enumerate(QKV_TILES):
                last = nc.vector.tensor_tensor(bq[0:m, t:t + 1], bq[0:m, t:t + 1], hid[0][0:m, t:t + 1], ALU.add)
            last.then_inc(s_bias, 1)
            dve.wait_ge(s_bias_mm, 2)
            nc.vector.tensor_tensor(b1[:, :], b1[:, :], hid[1][:, 0:MT], ALU.add).then_inc(s_bias, 1)

            def free(name, i, ins):
                ins.then_inc(s_bank[BANK_OF[name, i]], 1)

            def norm_stats(ln, name, s):
                for j, n in enumerate(CHUNKS[ln]):
                    c, cc = j // 2, j % 2
                    if cc == 0:
                        dve.wait_ge(s_pe[name], nth(s, 2, c))
                    nc.vector.bn_stats(st[ln][0:n, j, :], bank(name, c)[0:n, cc * C:(cc + 1) * C]).then_inc(s_stats[ln], 1)
                dve.wait_ge(s_stats[ln], nth(s, PAIRS, PAIRS - 1))
                dve.sem_inc(s_seen, 1)
                for j, n in enumerate(CHUNKS[ln]):
                    nc.vector.bn_aggr(mv[ln][0:n, j, :], st[ln][0:n, j, :]).then_inc(s_mv[ln], 1)

            def normalise(ln, name, s):
                dve.wait_ge(s_rs[ln], nth(s, 1, 0))
                for j, n in enumerate(CHUNKS[ln]):
                    c, cc = j // 2, j % 2
                    nc.vector.tensor_scalar(xn[0:n, j, :], bank(name, c)[0:n, cc * C:(cc + 1) * C], mv[ln][0:n, j, 0:1],
                                            rs[ln][0:n, j:j + 1], ALU.subtract, ALU.mult).then_inc(s_norm[ln], 1)
                    if cc == 1:
                        dve.wait_ge(s_norm[ln], nth(s, PAIRS, j))
                        dve.sem_inc(s_bank[BANK_OF[name, c]], 1)

            def lo_parts(name, psname, dst, s):
                dve.wait_ge(s_hi[name], nth(s, 2, 0))
                nc.vector.tensor_tensor(dst[1][:, :], bank(psname, 0)[:, 0:T], dst[0][:, :].bitcast(F32), ALU.subtract).then_inc(s_lo[name], 1)
                dve.wait_ge(s_hi[name], nth(s, 2, 1))
                nc.vector.tensor_tensor(dst[2][CR:128, :], bank(psname, 1)[0:CR, 0:T], dst[2][0:CR, :].bitcast(F32), ALU.subtract).then_inc(s_lo[name], 1)
                for i in range(2):
                    dve.wait_ge(s_lo[name], nth(s, 2, i))
                    dve.sem_inc(s_bank[BANK_OF[psname, i]], 1)

            def hidden_split(v, m):
                dve.wait_ge(s_gelu, nth(v, MT, m))
                if not isinstance(v, int) or MT * v + m >= 2:
                    dve.wait_ge(s_pe["fc2"], v * MT + (m - 1))
                nc.vector.tensor_copy(hh[:, m % 2, :], hf[:, m % 2, :]).then_inc(s_hh, 1)
                dve.wait_ge(s_hh, nth(v, MT, m))
                nc.vector.tensor_tensor(hl[:, m % 2, :], hf[:, m % 2, :], hh[:, m % 2, :].bitcast(F32), ALU.subtract).then_inc(s_hl, 1)

            def finish(v, k):
                dve.wait_ge(s_pe["fc2"], nth(v, MT, MT - 1))
                nc.vector.scalar_tensor_tensor(out=xt[:, k, 0, :], in0=yps[0][:, 0:T], scalar=b2[:, 0:1],
                                               in1=xt[:, k, 0, :], op0=ALU.add, op1=ALU.add).then_inc(s_fin, 1)
                dve.wait_ge(s_xr, nth(v, 1, 0))
                nc.vector.scalar_tensor_tensor(out=xt[0:CR, k, 1, :], in0=yps[1][0:CR, 0:T], scalar=b2[0:CR, 1:2],
                                               in1=xr[:, :], op0=ALU.add, op1=ALU.add).then_inc(s_fin, 1)

            def shift(s, i):
                (h0, h1), (j0, j1) = PARTS[i]
                if i == 0:
                    dve.wait_ge(s_pe["s"], nth(s, 1, 0))
                at = N * PAIRS * (h0 // 4)
                sc = att[0:SP, h0 % 4:h0 % 4 + h1 - h0, at:at + N * PAIRS].rearrange("p g (j m) -> p g j m", m=N)[:, :, j0:j1, :]
                nc.vector.reduce_max(rows(mx, i), sc, AX.X).then_inc(s_mx, 1)
                dve.wait_ge(s_mx, nth(s, 3, i))
                most = rows(mx, i).unsqueeze(3).to_broadcast([SP, h1 - h0, j1 - j0, N])
                nc.vector.tensor_tensor(probs(i), sc, most, ALU.subtract).then_inc(s_sub, 1)
                if i == 2:
                    dve.wait_ge(s_sub, nth(s, 3, 2))
                    for g in range(4):
                        dve.sem_inc(s_bank[g], 1)

            def sums(s, i):
                dve.wait_ge(s_exp, nth(s, 3, i))
                nc.vector.reduce_sum(rows(sm, i), probs(i), AX.X).then_inc(s_sum, 1)
                dve.wait_ge(s_sum, nth(s, 3, i))
                nc.vector.reciprocal(rows(rc, i), rows(sm, i)).then_inc(s_rec, 1)

            def v_blocks(s, c):
                dve.wait_ge(s_pe["vt"], nth(s, 2, c))
                src = bank("vt", c)[:, 0:2 * C].rearrange("p (j a d) -> p j a d", j=2, a=3)
                dst = vbd[:, 4 * c:4 * c + 4, :, :].rearrange("p (j w) a d -> p w j a d", w=2)
                for wi in range(2):
                    for e in range(2):
                        last = nc.vector.tensor_copy(dst[WP * e:WP * e + WP, wi, :, :, DH * e:DH * e + DH],
                                                     src[WP * wi:WP * wi + WP, :, :, DH * e:DH * e + DH])
                last.then_inc(s_vbd, 1)
                dve.wait_ge(s_vbd, nth(s, 2, c))
                dve.sem_inc(s_bank[BANK_OF["vt", c]], 1)

            def attention_and_mlp(s, k, it):
                v = s - 1
                mlp = not (isinstance(s, int) and s == 0)
                norm_stats(0, "ln1", s)
                if mlp:
                    hidden_split(v, 0)
                normalise(0, "ln1", s)
                if mlp:
                    hidden_split(v, 1)
                    hidden_split(v, 2)
                lo_parts("x1", "xn1", x1, s)
                for c in range(2):
                    v_blocks(s, c)
                shift(s, 0)
                shift(s, 1)
                sums(s, 0)
                shift(s, 2)
                sums(s, 1)
                sums(s, 2)
                if mlp:
                    hidden_split(v, 3)
                    hidden_split(v, 4)
                lo_parts("o", "o", o, s)
                norm_stats(1, "ln2", s)
                normalise(1, "ln2", s)
                if mlp:
                    hidden_split(v, 5)
                    finish(v, (k - 1) % SLOTS)
                lo_parts("x2", "xn2", x2, s)

            def last_mlp(v, k):
                for m in range(MT):
                    hidden_split(v, m)
                finish(v, k)

            steps(dve, attention_and_mlp, last_mlp)

        @block.gpsimd
        def _(pool):
            nc.gpsimd.memset(ident[:, :], 0.0).then_inc(s_id, 1)
            nc.gpsimd.memset(half[:, :], -0.5).then_inc(s_ve[0], 1)
            nc.gpsimd.memset(eps[:, :], EPS).then_inc(s_ve[0], 1)
            pool.wait_ge(s_id, 1)
            nc.gpsimd.affine_select(out=ident[:, :], in_=ident[:, :], compare_op=ALU.not_equal, fill=1.0,
                                    base=0, pattern=[[-1, 128]], channel_multiplier=1).then_inc(s_id, 1)
            pool.wait_ge(s_ve[0], 2)

            def rstd(ln, s):
                pool.wait_ge(s_mv[ln], nth(s, PAIRS, PAIRS - 1))
                n = max(CHUNKS[ln])
                nc.gpsimd.tensor_tensor(ve[ln][0:n, :], mv[ln][0:n, :, 1], eps[0:n, :], ALU.add).then_inc(s_ve[ln], 1)
                pool.wait_ge(s_ve[ln], nth(s, 1, 0) + (2 if ln == 0 else 0))
                nc.gpsimd.tensor_tensor(rs[ln][0:n, :], ve[ln][0:n, :], half[0:n, 0:PAIRS], ALU.pow).then_inc(s_rs[ln], 1)

            def residual(v, k):
                pool.wait_ge(s_ylo, nth(v, 1, 0))
                nc.gpsimd.tensor_tensor(xr[:, :], yl[:, :], xt[0:CR, k, 1, :], ALU.add).then_inc(s_xr, 1)

            def attention_and_mlp(s, k, it):
                rstd(0, s)
                for i in range(3):
                    pool.wait_ge(s_rec, nth(s, 3, i))
                    (h0, h1), (j0, j1) = PARTS[i]
                    each = rows(rc, i).unsqueeze(3).to_broadcast([SP, h1 - h0, j1 - j0, N])
                    nc.gpsimd.tensor_tensor(probs(i), probs(i), each, ALU.mult).then_inc(s_prob, 1)
                rstd(1, s)
                if not (isinstance(s, int) and s == 0):
                    residual(s - 1, (k - 1) % SLOTS)

            def last_mlp(v, k):
                residual(v, k)

            steps(pool, attention_and_mlp, last_mlp)


def kernel(x, L0_conv_norm1_w, L0_conv_norm1_b, L0_conv_qkv_w, L0_conv_qkv_b, L0_conv_proj_w, L0_conv_proj_b,
           L0_conv_norm2_w, L0_conv_norm2_b, L0_conv_fc1_w, L0_conv_fc1_b, L0_conv_fc2_w, L0_conv_fc2_b):
    import concourse.bacc as bacc
    from concourse.bass_utils import run_bass_kernel_spmd

    given = {
        "x": x, "norm1_w": L0_conv_norm1_w, "norm1_b": L0_conv_norm1_b,
        "qkv_wt": np.asarray(L0_conv_qkv_w).T, "qkv_b": L0_conv_qkv_b,
        "proj_wt": np.asarray(L0_conv_proj_w).T, "proj_b": L0_conv_proj_b,
        "norm2_w": L0_conv_norm2_w, "norm2_b": L0_conv_norm2_b,
        "fc1_wt": np.asarray(L0_conv_fc1_w).T, "fc1_b": L0_conv_fc1_b,
        "fc2_wt": np.asarray(L0_conv_fc2_w).T, "fc2_b": L0_conv_fc2_b,
    }
    nc = bacc.Bacc("TRN2", target_bir_lowering=False, num_devices=1)
    arrays, args = {}, []
    for name, a in given.items():
        a = np.ascontiguousarray(a)
        arrays[f"in_{name}"] = a
        args.append(nc.dram_tensor(f"in_{name}", a.shape, mybir.dt.from_np(a.dtype), kind="ExternalInput").ap())
    args.append(nc.dram_tensor("out", (B, C, H, W), F32, kind="ExternalOutput").ap())
    swin_block_program(nc, *args)
    return run_bass_kernel_spmd(nc, [arrays], core_ids=[0]).results[0]["out"]
```

```python
import numpy as np
import concourse.bass as bass
from concourse import mybir
from contextlib import ExitStack

F32 = mybir.dt.float32
F32R = mybir.dt.float32r
ALU = mybir.AluOpType
ACT = mybir.ActivationFunctionType
AX = mybir.AxisListType

B, C, H, W = 16, 192, 56, 56
WIN, SHIFT, HEADS = 7, 3, 6
DH = C // HEADS
HID = 4 * C
N = WIN * WIN
NW = W // WIN
T = NW * N
UPB = H // WIN
UNITS = B * UPB
CM = 128
CR = C - CM
MT = HID // 128
PAIRS = NW // 2
TP = 2 * N
WP = 64
SP = WP + N
ROWS = [2, 2, 2, 1]
CHUNKS = [[W * r for r in ROWS], [TP] * PAIRS]
TM = max(CHUNKS[0])
SLOTS = 4
SCALE = float(DH) ** -0.5
EPS = 1e-5

PA = 4 * W - SHIFT
PB = T - SHIFT
SMALL = 16 * (12 + 6 + 4 + MT)
LOADS = 6

BANK_USES = [("x2", 0, 3), ("x2", 1, 0), ("ln1", 0, 1), ("ln1", 1, 2),
             ("s", 0, 3), ("s", 1, 0), ("s", 2, 3), ("s", 3, 0), ("x1", 0, 1), ("x1", 1, 2),
             ("qkv", 0, 1), ("qkv", 1, 2), ("pt", 0, 3), ("pt", 1, 0), ("o", 0, 1), ("o", 1, 2),
             ("pt", 2, 3), ("pt", 3, 0), ("proj", 0, 1), ("proj", 1, 2), ("vt", 0, 3), ("vt", 1, 0),
             ("qkv", 4, 3), ("ln2", 0, 1), ("ln2", 1, 2), ("qkv", 2, 0), ("qkv", 3, 3)]
BANK_OF = {(n, i): b for n, i, b in BANK_USES}
LAG = {"x2": 2, "ln1": 0, "x1": 0, "qkv": 0, "vt": 0, "s": 1, "pt": 1, "o": 1, "proj": 1, "ln2": 1}


def use_before(name, part, t):
    b = BANK_OF[name, part]
    own = [(n, i) for n, i, bank in BANK_USES if bank == b]
    at = own.index((name, part))
    for back in range(1, 4 * len(own)):
        n, i = own[(at - back) % len(own)]
        v = t - (LAG[n] + (back - at + len(own) - 1) // len(own))
        if not isinstance(v, int) or 0 <= v < UNITS:
            return n, i, v
    return None


QKV_COLS = [(2 * C, CM), (2 * C + CM, CR), (0, CM), (C, CM), (CM, CR), (C + CM, CR)]
QKV_TILES = [(0, 128), (128, 64), (192, 128), (320, 128), (448, 128)]


QKV_READS = [1, 2, 6, 10, 5, 10]


def nth(unit, per_unit, i):
    return unit * per_unit + (i + 1)


def swin_block_program(nc, x, n1w, n1b, qkv_wt, qkv_b, proj_wt, proj_b, n2w, n2b,
                       fc1_wt, fc1_b, fc2_wt, fc2_b, out):
    ctx = ExitStack()
    with ctx:
        def sb(name, shape, dt=F32):
            return ctx.enter_context(nc.sbuf_tensor(name, shape, dt))

        def sem(name):
            return ctx.enter_context(nc.semaphore(name))

        ident = sb("ident", [128, 128])
        half = sb("half", [128, PAIRS])
        eps = sb("eps", [128, PAIRS])
        NQ, NF = 3 * C, HID
        wq = [sb(f"wq_{p}", [128, NQ], F32R) for p in ("mh", "ml", "rh", "rl")]
        wp = [sb(f"wp_{p}", [128, C], F32R) for p in ("mh", "ml", "rh", "rl")]
        w1 = [sb(f"w1_{p}", [128, NF], F32R) for p in ("mh", "ml", "rh", "rl")]
        w2h = sb("w2h", [128, MT, C], F32R)
        w2l = sb("w2l", [128, MT, CM], F32R)
        w2r = sb("w2r", [128, MT, 128], F32R)
        bq = sb("bq", [128, 5])
        bp = sb("bp", [128, 2])
        b1 = sb("b1", [128, MT])
        b2 = sb("b2", [128, 2])
        raw_m = sb("raw_m", [128, NF])
        raw_r = sb("raw_r", [128, NF])
        raw_2 = sb("raw_2", [128, MT, C])
        scl_m = sb("scl_m", [128, NF])
        scl_r = sb("scl_r", [128, NF])
        nwb = sb("nwb", [128, 8])

        xt = sb("xt", [128, SLOTS, 2, T])
        st = [sb(f"st{i}", [TM, PAIRS, 6]) for i in range(2)]
        mv = [sb(f"mv{i}", [TM, PAIRS, 2]) for i in range(2)]
        ve = [sb(f"ve{i}", [TM, PAIRS]) for i in range(2)]
        rs = [sb(f"rs{i}", [TM, PAIRS]) for i in range(2)]
        xn = sb("xn", [TM, PAIRS, C])
        x1 = [sb(f"x1_{p}", [128, T], F32R) for p in ("h", "l", "r")]
        x2 = [sb(f"x2_{p}", [128, T], F32R) for p in ("h", "l", "r")]
        qm = sb("qm", [128, T])
        km = sb("km", [128, NW, 4 * N])
        qr = sb("qr", [CR, T])
        kr = sb("kr", [CR, NW, 2 * N])
        vm = sb("vm", [128, NW, WP])
        vr = sb("vr", [CR, NW, WP])
        vbd = sb("vbd", [128, NW, 3, WP])
        pr = sb("pr", [SP, PAIRS, HEADS * WP])
        mx = sb("mx", [SP, PAIRS, HEADS])
        sm = sb("sm", [SP, PAIRS, HEADS])
        rc = sb("rc", [SP, PAIRS, HEADS])
        pt = sb("pt", [SP, 2, 3, 128])
        o = [sb(f"o_{p}", [128, T], F32R) for p in ("h", "l", "r")]
        pj = sb("pj", [128, 2, T])
        hf = sb("hf", [128, 2, T])
        hh = sb("hh", [128, 2, T], F32R)
        hl = sb("hl", [128, 2, T], F32R)
        yl = sb("yl", [CR, T])
        yr = sb("yr", [CR, T])

        att = ctx.enter_context(nc.psum_tensor("att", [128, 4, 512], F32))
        hid = [ctx.enter_context(nc.psum_tensor(f"hid{i}", [128, 512], F32)) for i in range(2)]
        yps = [ctx.enter_context(nc.psum_tensor(f"yps{i}", [128, 512], F32)) for i in range(2)]

        HI_LO = {"x1": x1, "x2": x2, "o": o}

        def bank(name, i):
            return att[:, BANK_OF[name, i], :]

        s_raw = [sem(f"raw_loaded_{i}") for i in range(4)]
        s_small = sem("small_loaded")
        s_id = sem("ident_made")
        s_zero = sem("pads_zeroed")
        s_scaled = sem("weights_scaled")
        s_split = sem("weights_split")
        s_rawfree = sem("raw_used_by_bias_products")
        s_bias_mm = sem("bias_products_done")
        s_bias = sem("biases_ready")
        s_x = [sem(f"x_loaded_{i}") for i in range(SLOTS)]
        s_st = [sem(f"out_stored_{i}") for i in range(SLOTS)]
        s_pe = {n: sem(f"pe_{n}") for n in ("ln1", "x1", "qkv", "vt", "s", "pt", "o", "proj", "ln2", "x2", "fc1", "fc2")}
        s_stats = [sem(f"bn_stats_done_{i}") for i in range(2)]
        s_seen = sem("bn_stats_seen")
        s_mv = [sem(f"mean_var_done_{i}") for i in range(2)]
        s_ve = [sem(f"var_eps_done_{i}") for i in range(2)]
        s_rs = [sem(f"rstd_done_{i}") for i in range(2)]
        s_norm = [sem(f"normalised_{i}") for i in range(2)]
        s_hi = {n: sem(f"hi_{n}") for n in ("x1", "x2", "o")}
        s_lo = {n: sem(f"lo_{n}") for n in ("x1", "x2", "o")}
        s_qkv = sem("qkv_in_sbuf")
        s_vbd = sem("vbd_ready")
        s_mx = sem("row_max")
        s_sub = sem("max_subtracted")
        s_exp = sem("exp_done")
        s_sum = sem("row_sum")
        s_rec = sem("sum_reciprocal")
        s_prob = sem("probabilities")
        s_ptc = sem("pt_in_sbuf")
        s_pj = sem("proj_in_sbuf")
        s_gelu = sem("gelu_done")
        s_hh = sem("hidden_hi")
        s_hl = sem("hidden_lo")
        s_ylo = sem("y_rem_lo_copied")
        s_ym = sem("out_main_ready")
        s_yr = sem("y_rem_summed")
        s_or = sem("out_rem_ready")

        xf = x.rearrange("b c h w -> b c (h w)")
        of = out.rearrange("b c h w -> b c (h w)")

        def runs(i):
            a = i * T + SHIFT * W + SHIFT
            b = (a + PA) % (H * W)
            return [(a, PA, 0), (b, PB - PA, PA), (a - SHIFT, SHIFT, PB)]

        def rows_by_window(ap, j):
            r0, n = sum(ROWS[:j]), ROWS[j]
            return ap.rearrange("p (w r c) -> p r w c", r=WIN, w=NW)[:, r0:r0 + n]

        def windows_by_row(ap, j):
            return ap.rearrange("p (r w c) -> p w r c", r=WIN, w=NW)[:, 2 * j:2 * j + 2]

        def last_read(name, i, v):
            if name in ("x1", "x2", "o"):
                return s_lo[name], nth(v, 2, i)
            if name in ("ln1", "ln2"):
                return s_norm[name == "ln2"], nth(v, PAIRS, 2 * i + 1)
            if name == "qkv":
                return s_qkv, nth(v, QKV_READS[-1], QKV_READS[i] - 1)
            return {"vt": (s_vbd, nth(v, 2, i)), "s": (s_sub, nth(v, PAIRS, i)), "pt": (s_ptc, nth(v, PAIRS, i)),
                    "proj": (s_pj, nth(v, 2, i))}[name]

        def probs(j):
            return pr[:, j, :].rearrange("p (h m) -> p h m", h=HEADS)[:, :, 0:N]

        def five(ps, w, c0, m, act, n=T):
            wmh, wml, wrh, wrl = w
            xh, xl, xrr = act
            nc.tensor.matmul(ps, wmh[:, c0:c0 + m], xh[:, :], start=True, stop=False)
            nc.tensor.matmul(ps, wml[:, c0:c0 + m], xh[:, :], start=False, stop=False)
            nc.tensor.matmul(ps, wmh[:, c0:c0 + m], xl[:, :], start=False, stop=False)
            nc.tensor.matmul(ps, wrh[:, c0:c0 + m], xrr[:, :], start=False, stop=False)
            return nc.tensor.matmul(ps, wrl[:, c0:c0 + m], xrr[:, :], start=False, stop=True)

        block = ctx.enter_context(nc.Block())

        @block.sync
        def _(sp):
            def load(b, i):
                u = b * UPB + i
                slot = i % SLOTS
                if not (isinstance(u, int) and u < SLOTS):
                    sp.wait_ge(s_st[slot], (b * 2 + i // SLOTS) * (16 * LOADS))
                for px, n, at in runs(i):
                    sp.dma_start(xt[:, slot, 0, at:at + n], xf[b, 0:CM, px:px + n]).then_inc(s_x[slot], 16)
                    sp.dma_start(xt[0:CR, slot, 1, at:at + n], xf[b, CM:C, px:px + n]).then_inc(s_x[slot], 16)

            def store(b, i):
                slot = i % SLOTS
                sp.wait_ge(s_ym, b * UPB + (i + 1))
                sp.wait_ge(s_or, b * UPB + (i + 1))
                for px, n, at in runs(i):
                    sp.dma_start(of[b, 0:CM, px:px + n], xt[:, slot, 0, at:at + n]).then_inc(s_st[slot], 16)
                    sp.dma_start(of[b, CM:C, px:px + n], xt[0:CR, slot, 1, at:at + n]).then_inc(s_st[slot], 16)

            for k, (vec, cols) in enumerate(((n1w, 0), (n1b, 2), (n2w, 4), (n2b, 6))):
                sp.dma_start(nwb[:, cols:cols + 1], vec[0:CM].rearrange("(p a) -> p a", a=1)).then_inc(s_small, 16)
                for h in range(2):
                    sp.dma_start(nwb[h * CR:(h + 1) * CR, cols + 1:cols + 2],
                                 vec[CM:C].rearrange("(p a) -> p a", a=1)).then_inc(s_small, 16)
            at = 0
            for c0, m in QKV_COLS:
                t, r = next((k, at - s) for k, (s, n) in enumerate(QKV_TILES) if s <= at < s + n)
                sp.dma_start(bq[r:r + m, t:t + 1], qkv_b[c0:c0 + m].rearrange("(p a) -> p a", a=1)).then_inc(s_small, 16)
                at += m
            for vec, dst in ((proj_b, bp), (fc2_b, b2)):
                sp.dma_start(dst[:, 0:1], vec[0:CM].rearrange("(p a) -> p a", a=1)).then_inc(s_small, 16)
                sp.dma_start(dst[0:CR, 1:2], vec[CM:C].rearrange("(p a) -> p a", a=1)).then_inc(s_small, 16)
            for m in range(MT):
                sp.dma_start(b1[:, m:m + 1], fc1_b[m * 128:(m + 1) * 128].rearrange("(p a) -> p a", a=1)).then_inc(s_small, 16)
            at = 0
            for c0, m in QKV_COLS:
                sp.dma_start(raw_m[:, at:at + m], qkv_wt[0:CM, c0:c0 + m]).then_inc(s_raw[0], 16)
                for h in range(2):
                    sp.dma_start(raw_r[h * CR:(h + 1) * CR, at:at + m], qkv_wt[CM:C, c0:c0 + m]).then_inc(s_raw[0], 16)
                at += m
            load(0, 0)
            sp.dma_start(raw_2[:, :, :], fc2_wt.rearrange("(m p) n -> p m n", p=128)).then_inc(s_raw[3], 16)
            for n, (wt, cols) in enumerate(((proj_wt, C), (fc1_wt, NF))):
                sp.wait_ge(s_rawfree, n + 1)
                sp.dma_start(raw_m[:, 0:cols], wt[0:CM, :]).then_inc(s_raw[n + 1], 16)
                for h in range(2):
                    sp.dma_start(raw_r[h * CR:(h + 1) * CR, 0:cols], wt[CM:C, :]).then_inc(s_raw[n + 1], 16)

            def step(b, i):
                if i >= 3:
                    store(b, i - 3)
                elif not (isinstance(b, int) and b == 0):
                    store(b - 1, UPB - 3 + i)
                if i < UPB - 1:
                    load(b, i + 1)
                elif not (isinstance(b, int) and b == B - 1):
                    load(b + 1, 0)

            for i in range(UPB):
                step(0, i)
            with sp.Fori(1, B - 1) as b:
                for i in range(UPB):
                    step(b, i)
            for i in range(UPB):
                step(B - 1, i)
            for i in range(3):
                store(B - 1, UPB - 3 + i)
            for slot in range(SLOTS):
                sp.wait_ge(s_st[slot], 16 * LOADS * (UNITS // SLOTS))

        def steps(eng, step):
            for t in range(SLOTS):
                step(t, t, 0)
            with eng.Fori(1, UNITS // SLOTS) as it:
                for k in range(SLOTS):
                    step(it * SLOTS + k, k, it)
            for t in range(UNITS, UNITS + 3):
                step(t, t % SLOTS, t // SLOTS)

        def streams(t):
            return [not isinstance(t, int) or 0 <= t - lag < UNITS for lag in range(4)]

        @block.tensor
        def _(pe):
            pe.wait_ge(s_id, 2)
            pe.wait_ge(s_small, SMALL)

            def claim(name, i, t):
                use = use_before(name, i, t)
                if use is not None:
                    pe.wait_ge(*last_read(*use))

            pe.wait_ge(s_raw[0], 16 * 18)
            for t, (c0, m) in enumerate(QKV_TILES):
                nc.tensor.matmul(hid[0][0:m, t:t + 1], raw_m[:, c0:c0 + m], nwb[:, 2:3], start=True, stop=False)
                last = nc.tensor.matmul(hid[0][0:m, t:t + 1], raw_r[0:CR, c0:c0 + m], nwb[0:CR, 3:4], start=False, stop=True)
            last.then_inc(s_bias_mm, 1)
            pe.wait_ge(s_raw[2], 16 * 3)
            for m in range(MT):
                nc.tensor.matmul(hid[1][:, m:m + 1], raw_m[:, m * 128:(m + 1) * 128], nwb[:, 6:7], start=True, stop=False)
                last = nc.tensor.matmul(hid[1][:, m:m + 1], raw_r[0:CR, m * 128:(m + 1) * 128], nwb[0:CR, 7:8], start=False, stop=True)
            last.then_inc(s_bias_mm, 1)
            pe.wait_ge(s_zero, 1)
            pe.wait_ge(s_split, 4)
            pe.wait_ge(s_bias, 2)

            def to_tokens(name, ln, t, tile_m, tile_r):
                for j, n in enumerate(CHUNKS[ln]):
                    c, cc = j // 2, j % 2
                    if cc == 0:
                        claim(name, c, t)
                    at = sum(CHUNKS[ln][:j])
                    ps = bank(name, c)[0:n, cc * C:(cc + 1) * C]
                    nc.tensor.transpose(ps[:, 0:CM], tile_m[:, at:at + n], ident[:, :])
                    last = nc.tensor.transpose(ps[:, CM:C], tile_r[:, at:at + n], ident[0:CR, 0:CR])
                    if cc == 1:
                        last.then_inc(s_pe[name], 1)

            def to_channels(name, ln, t, v, place):
                claim(name, 0, t)
                claim(name, 1, t)
                for g, (c0, m) in enumerate(((0, CM), (CM, CR))):
                    for j, n in enumerate(CHUNKS[ln]):
                        if g == 0 and j < 3:
                            pe.wait_ge(s_norm[ln], nth(v, PAIRS, j + (j == 2)))
                        last = nc.tensor.transpose(place(bank(name, g)[0:m, 0:T], j), xn[0:n, j, c0:c0 + m], ident[0:n, 0:n])
                    last.then_inc(s_pe[name], 1)

            def fc1(v, m):
                if m == 0:
                    pe.wait_ge(s_lo["x2"], nth(v, 2, 1))
                if not isinstance(v, int) or MT * v + m >= 2:
                    pe.wait_ge(s_gelu, v * MT + (m - 1))
                five(hid[m % 2][:, 0:T], w1, m * 128, 128, x2).then_inc(s_pe["fc1"], 1)

            def fc2(v, m):
                pe.wait_ge(s_hl, nth(v, MT, m))
                if m == 0 and not (isinstance(v, int) and v == 0):
                    pe.wait_ge(s_yr, v)
                a, z = m == 0, m == MT - 1
                b = m % 2
                ym, yx = yps[0][:, 0:T], yps[1][:, 0:T]
                nc.tensor.matmul(ym, w2h[:, m, 0:CM], hh[:, b, :], start=a, stop=False)
                nc.tensor.matmul(ym, w2l[:, m, :], hh[:, b, :], start=False, stop=False)
                nc.tensor.matmul(yx, w2r[:, m, :], hh[:, b, :], start=a, stop=z, skip_group_check=True)
                nc.tensor.matmul(ym, w2h[:, m, 0:CM], hl[:, b, :], start=False, stop=z)
                nc.tensor.matmul(yx[0:CR], w2h[:, m, CM:C], hl[:, b, :], start=False, stop=z,
                                 skip_group_check=True).then_inc(s_pe["fc2"], 1)

            def scores(t, v, j):
                claim("s", j, t)
                for wi in range(2):
                    w = 2 * j + wi
                    rows = bank("s", j)[WP * wi:WP * wi + N, :]
                    nc.tensor.matmul(rows[:, 0:4 * N], qm[:, N * w:N * w + N], km[:, w, :], start=True, stop=True)
                    last = nc.tensor.matmul(rows[:, 4 * N:6 * N], qr[:, N * w:N * w + N], kr[:, w, :], start=True, stop=True)
                last.then_inc(s_pe["s"], 1)

            def probs_t(t, v, j):
                claim("pt", j, t)
                pe.wait_ge(s_prob, nth(v, PAIRS, j))
                for p in range(3):
                    last = nc.tensor.transpose(bank("pt", j)[0:SP, 128 * p:128 * p + SP],
                                               pr[:, j, 2 * WP * p:2 * WP * p + SP], ident[0:SP, 0:SP])
                last.then_inc(s_pe["pt"], 1)

            def weighted(t, v, j):
                if j == 0:
                    pe.wait_ge(s_vbd, nth(v, 2, 1))
                    claim("o", 0, t)
                    claim("o", 1, t)
                pe.wait_ge(s_ptc, nth(v, PAIRS, j))
                for wi in range(2):
                    w = 2 * j + wi
                    for p in range(3):
                        ps = bank("o", p // 2)[WP * (p % 2):WP * (p % 2) + WP, N * w:N * w + N]
                        last = nc.tensor.matmul(ps, vbd[0:SP, w, p, :], pt[:, j % 2, p, WP * wi:WP * wi + N],
                                                start=True, stop=True)
                if j == PAIRS - 1:
                    last.then_inc(s_pe["o"], 1)

            def qkv(t, tile):
                c0, m = QKV_TILES[tile]
                claim("qkv", tile, t)
                five(bank("qkv", tile)[0:m, 0:T], wq, c0, m, x1).then_inc(s_pe["qkv"], 1)

            def v_to_keys(t):
                pe.wait_ge(s_qkv, nth(t, QKV_READS[-1], QKV_READS[1] - 1))
                for j in range(PAIRS):
                    c, cc = j // 2, j % 2
                    if cc == 0:
                        claim("vt", c, t)
                    ps = bank("vt", c)[:, cc * C:(cc + 1) * C]
                    for src, m, c0 in ((vm, CM, 0), (vr, CR, CM)):
                        pair = src[0:m, 2 * j:2 * j + 2, :].rearrange("p w n -> p (w n)")
                        last = nc.tensor.transpose(ps[:, c0:c0 + m], pair, ident[0:m, 0:m])
                    if cc == 1:
                        last.then_inc(s_pe["vt"], 1)

            def step(t, k, it):
                X, Y, Z, E = streams(t)
                y, z, e = t - 1, t - 2, t - 3
                if Z:
                    to_channels("x2", 1, t, z, windows_by_row)
                if X:
                    pe.wait_ge(s_x[k], (it + 1) * (16 * LOADS))
                    to_tokens("ln1", 0, t, xt[:, k, 0, :], xt[0:CR, k, 1, :])
                if E:
                    fc2(e, 4)
                    fc2(e, 5)
                if Y:
                    pe.wait_ge(s_qkv, nth(y, QKV_READS[-1], QKV_READS[-1] - 1))
                    scores(t, y, 0)
                    scores(t, y, 1)
                if Z:
                    fc1(z, 0)
                    fc1(z, 1)
                if Y:
                    scores(t, y, 2)
                    scores(t, y, 3)
                if X:
                    to_channels("x1", 0, t, t, rows_by_window)
                if Z:
                    fc2(z, 0)
                    fc1(z, 2)
                if X:
                    pe.wait_ge(s_lo["x1"], nth(t, 2, 1))
                    qkv(t, 0)
                    qkv(t, 1)
                if Y:
                    probs_t(t, y, 0)
                    probs_t(t, y, 1)
                    weighted(t, y, 0)
                    probs_t(t, y, 2)
                    weighted(t, y, 1)
                    probs_t(t, y, 3)
                    weighted(t, y, 2)
                    weighted(t, y, 3)
                if Z:
                    fc2(z, 1)
                    fc1(z, 3)
                if Y:
                    pe.wait_ge(s_lo["o"], nth(y, 2, 1))
                    for i, (c0, m) in enumerate(((0, CM), (CM, CR))):
                        claim("proj", i, t)
                        five(bank("proj", i)[0:m, 0:T], wp, c0, m, o).then_inc(s_pe["proj"], 1)
                if X:
                    v_to_keys(t)
                    qkv(t, 4)
                if Y:
                    pe.wait_ge(s_pj, nth(y, 2, 1))
                    to_tokens("ln2", 1, t, pj[:, 0, :], pj[0:CR, 1, :])
                if X:
                    qkv(t, 2)
                    qkv(t, 3)
                if Z:
                    fc2(z, 2)
                    fc1(z, 4)
                    fc2(z, 3)
                    fc1(z, 5)

            steps(pe, step)

        @block.scalar
        def _(act):
            act.wait_ge(s_zero, 1)
            act.wait_ge(s_bias, 2)

            def copy(dst, src, done):
                nc.scalar.activation(dst, src, ACT.Copy).then_inc(done, 1)

            def biased(dst, src, bias, done):
                return nc.scalar.activation(dst, src, ACT.Identity, bias=bias).then_inc(done, 1)

            def hi_parts(name, v, signals):
                for i, (dst, m) in enumerate(((0, CM), (2, CR))):
                    if i < signals:
                        act.wait_ge(s_pe[name], nth(v, signals, i))
                    copy(HI_LO[name][dst][0:m, :], bank(name, i)[0:m, 0:T], s_hi[name])

            def gelu(v, m):
                act.wait_ge(s_pe["fc1"], nth(v, MT, m))
                if not isinstance(v, int) or MT * v + m >= 2:
                    act.wait_ge(s_hl, v * MT + (m - 1))
                nc.scalar.activation(hf[:, m % 2, :], hid[m % 2][:, 0:T], ACT.Gelu, bias=b1[:, m:m + 1]).then_inc(s_gelu, 1)

            def y_low(v):
                act.wait_ge(s_pe["fc2"], nth(v, MT, MT - 1))
                copy(yl[:, :], yps[1][CR:128, 0:T], s_ylo)

            def exps(v, j):
                act.wait_ge(s_sub, nth(v, PAIRS, j))
                nc.scalar.activation(probs(j), probs(j), ACT.Exp, scale=SCALE).then_inc(s_exp, 1)

            def pt_copy(v, j):
                act.wait_ge(s_pe["pt"], nth(v, PAIRS, j))
                src = bank("pt", j)[0:SP, 0:384].rearrange("p (a m) -> p a m", a=3)[:, :, 0:SP]
                copy(pt[:, j % 2, :, 0:SP], src, s_ptc)

            by_window = km.rearrange("p w (h n) -> p w h n", h=4)
            by_window_r = kr.rearrange("p w (h n) -> p w h n", h=2)
            places = {0: [(vm[:, :, 0:N], 0, CM)], 1: [(vr[:, :, 0:N], 0, CR)],
                      2: [(qm.rearrange("p (w n) -> p w n", w=NW), 0, CM)],
                      3: [(by_window[DH * h:DH * h + DH, :, h, :], DH * h, DH) for h in range(4)],
                      4: [(qr.rearrange("p (w n) -> p w n", w=NW), 0, CR)]
                         + [(by_window_r[DH * h:DH * h + DH, :, h, :], CR + DH * h, DH) for h in range(2)]}

            def qkv_out(v, i, tile):
                act.wait_ge(s_pe["qkv"], nth(v, 5, i))
                for dst, r, m in places[tile]:
                    src = bank("qkv", tile)[r:r + m, 0:T].rearrange("p (w n) -> p w n", w=NW)
                    biased(dst, src, bq[r:r + m, tile:tile + 1], s_qkv)

            def step(t, k, it):
                X, Y, Z, E = streams(t)
                y, z, e = t - 1, t - 2, t - 3
                if Z:
                    hi_parts("x2", z, 2)
                if E:
                    y_low(e)
                if Z:
                    gelu(z, 0)
                    gelu(z, 1)
                if Y:
                    exps(y, 0)
                    exps(y, 1)
                if X:
                    hi_parts("x1", t, 2)
                if Y:
                    exps(y, 2)
                    exps(y, 3)
                if Z:
                    gelu(z, 2)
                if X:
                    qkv_out(t, 0, 0)
                    qkv_out(t, 1, 1)
                if Y:
                    for j in range(PAIRS):
                        pt_copy(y, j)
                    hi_parts("o", y, 1)
                if Z:
                    gelu(z, 3)
                if Y:
                    for i, m in enumerate((CM, CR)):
                        act.wait_ge(s_pe["proj"], nth(y, 2, i))
                        biased(pj[0:m, i, :], bank("proj", i)[0:m, 0:T], bp[0:m, i:i + 1], s_pj)
                if X:
                    qkv_out(t, 2, 4)
                    qkv_out(t, 3, 2)
                    qkv_out(t, 4, 3)
                if Z:
                    gelu(z, 4)
                    gelu(z, 5)

            steps(act, step)

        @block.vector
        def _(dve):
            for t in (vm, vr, km, kr, vbd, pr, pt, mv[0], mv[1]):
                nc.vector.memset(t[:], 0.0)
            nc.vector.memset(att[:, :, :], 0.0).then_inc(s_zero, 1)

            scaled = split = 0
            dve.wait_ge(s_small, SMALL)
            for n, (w, cols, nw) in enumerate(((wq, NQ, 0), (wp, C, None), (w1, NF, 4))):
                dve.wait_ge(s_raw[n], 16 * (18 if n == 0 else 3))
                sm_, sr_ = raw_m, raw_r
                if nw is not None:
                    if n:
                        dve.wait_ge(s_split, n)
                    nc.vector.tensor_scalar(scl_m[:, 0:cols], raw_m[:, 0:cols], nwb[:, nw:nw + 1], None, ALU.mult).then_inc(s_scaled, 1)
                    nc.vector.tensor_scalar(scl_r[:, 0:cols], raw_r[:, 0:cols], nwb[:, nw + 1:nw + 2], None, ALU.mult).then_inc(s_scaled, 1)
                    scaled += 2
                    dve.wait_ge(s_scaled, scaled)
                    sm_, sr_ = scl_m, scl_r
                nc.vector.tensor_copy(w[0][:, :], sm_[:, 0:cols]).then_inc(s_scaled, 1)
                nc.vector.tensor_copy(w[2][:, :], sr_[:, 0:cols]).then_inc(s_scaled, 1)
                scaled += 2
                dve.wait_ge(s_scaled, scaled)
                nc.vector.tensor_tensor(w[1][:, :], sm_[:, 0:cols], w[0][:, :].bitcast(F32), ALU.subtract)
                nc.vector.tensor_tensor(w[3][:, :], sr_[:, 0:cols], w[2][:, :].bitcast(F32), ALU.subtract).then_inc(s_split, 1)
                if n < 2:
                    if n == 0:
                        dve.wait_ge(s_bias_mm, 1)
                    dve.wait_ge(s_split, n + 1)
                    dve.sem_inc(s_rawfree, 1)
            dve.wait_ge(s_raw[3], 16)
            nc.vector.tensor_copy(w2h[:, :, :], raw_2[:, :, :]).then_inc(s_scaled, 1)
            nc.vector.tensor_copy(w2r[:, :, 0:CR], raw_2[:, :, CM:C]).then_inc(s_scaled, 1)
            dve.wait_ge(s_scaled, scaled + 2)
            nc.vector.tensor_tensor(w2l[:, :, :], raw_2[:, :, 0:CM], w2h[:, :, 0:CM].bitcast(F32), ALU.subtract)
            nc.vector.tensor_tensor(w2r[:, :, CR:128], raw_2[:, :, CM:C], w2r[:, :, 0:CR].bitcast(F32), ALU.subtract).then_inc(s_split, 1)
            dve.wait_ge(s_bias_mm, 1)
            for t, (c0, m) in enumerate(QKV_TILES):
                last = nc.vector.tensor_tensor(bq[0:m, t:t + 1], bq[0:m, t:t + 1], hid[0][0:m, t:t + 1], ALU.add)
            last.then_inc(s_bias, 1)
            dve.wait_ge(s_bias_mm, 2)
            nc.vector.tensor_tensor(b1[:, :], b1[:, :], hid[1][:, 0:MT], ALU.add).then_inc(s_bias, 1)

            def norm_stats(ln, name, s):
                for j, n in enumerate(CHUNKS[ln]):
                    c, cc = j // 2, j % 2
                    if cc == 0:
                        dve.wait_ge(s_pe[name], nth(s, 2, c))
                    nc.vector.bn_stats(st[ln][0:n, j, :], bank(name, c)[0:n, cc * C:(cc + 1) * C]).then_inc(s_stats[ln], 1)
                dve.wait_ge(s_stats[ln], nth(s, PAIRS, PAIRS - 1))
                dve.sem_inc(s_seen, 1)
                for j, n in enumerate(CHUNKS[ln]):
                    nc.vector.bn_aggr(mv[ln][0:n, j, :], st[ln][0:n, j, :]).then_inc(s_mv[ln], 1)

            def normalise(ln, name, s):
                dve.wait_ge(s_rs[ln], nth(s, 1, 0))
                for j, n in enumerate(CHUNKS[ln]):
                    c, cc = j // 2, j % 2
                    nc.vector.tensor_scalar(xn[0:n, j, :], bank(name, c)[0:n, cc * C:(cc + 1) * C], mv[ln][0:n, j, 0:1],
                                            rs[ln][0:n, j:j + 1], ALU.subtract, ALU.mult).then_inc(s_norm[ln], 1)

            def lo_parts(name, v):
                xh, xl, xrr = HI_LO[name]
                dve.wait_ge(s_hi[name], nth(v, 2, 0))
                nc.vector.tensor_tensor(xl[:, :], bank(name, 0)[:, 0:T], xh[:, :].bitcast(F32), ALU.subtract).then_inc(s_lo[name], 1)
                dve.wait_ge(s_hi[name], nth(v, 2, 1))
                nc.vector.tensor_tensor(xrr[CR:128, :], bank(name, 1)[0:CR, 0:T], xrr[0:CR, :].bitcast(F32), ALU.subtract).then_inc(s_lo[name], 1)

            def hidden_split(v, m):
                dve.wait_ge(s_gelu, nth(v, MT, m))
                if not isinstance(v, int) or MT * v + m >= 2:
                    dve.wait_ge(s_pe["fc2"], v * MT + (m - 1))
                nc.vector.tensor_copy(hh[:, m % 2, :], hf[:, m % 2, :]).then_inc(s_hh, 1)
                dve.wait_ge(s_hh, nth(v, MT, m))
                nc.vector.tensor_tensor(hl[:, m % 2, :], hf[:, m % 2, :], hh[:, m % 2, :].bitcast(F32), ALU.subtract).then_inc(s_hl, 1)

            def finish(v, k):
                dve.wait_ge(s_pe["fc2"], nth(v, MT, MT - 1))
                nc.vector.scalar_tensor_tensor(out=xt[:, k, 0, :], in0=yps[0][:, 0:T], scalar=b2[:, 0:1],
                                               in1=xt[:, k, 0, :], op0=ALU.add, op1=ALU.add).then_inc(s_ym, 1)
                dve.wait_ge(s_ylo, nth(v, 1, 0))
                if not (isinstance(v, int) and v == 0):
                    dve.wait_ge(s_or, v)
                nc.vector.scalar_tensor_tensor(out=yr[:, :], in0=yps[1][0:CR, 0:T], scalar=b2[0:CR, 1:2],
                                               in1=yl[:, :], op0=ALU.add, op1=ALU.add).then_inc(s_yr, 1)

            def shift(v, j):
                dve.wait_ge(s_pe["s"], nth(v, PAIRS, j))
                sc = bank("s", j)[0:SP, 0:HEADS * N].rearrange("p (h m) -> p h m", m=N)
                nc.vector.reduce_max(mx[:, j, :], sc, AX.X).then_inc(s_mx, 1)
                dve.wait_ge(s_mx, nth(v, PAIRS, j))
                most = mx[:, j, :].unsqueeze(2).to_broadcast([SP, HEADS, N])
                nc.vector.tensor_tensor(probs(j), sc, most, ALU.subtract).then_inc(s_sub, 1)

            def sums(v, j):
                dve.wait_ge(s_exp, nth(v, PAIRS, j))
                nc.vector.reduce_sum(sm[:, j, :], probs(j), AX.X).then_inc(s_sum, 1)
                dve.wait_ge(s_sum, nth(v, PAIRS, j))
                nc.vector.reciprocal(rc[:, j, :], sm[:, j, :]).then_inc(s_rec, 1)

            def v_blocks(s, c):
                dve.wait_ge(s_pe["vt"], nth(s, 2, c))
                src = bank("vt", c)[:, 0:2 * C].rearrange("p (j a d) -> p j a d", j=2, a=3)
                dst = vbd[:, 4 * c:4 * c + 4, :, :].rearrange("p (j w) a d -> p w j a d", w=2)
                for wi in range(2):
                    for e in range(2):
                        last = nc.vector.tensor_copy(dst[WP * e:WP * e + WP, wi, :, :, DH * e:DH * e + DH],
                                                     src[WP * wi:WP * wi + WP, :, :, DH * e:DH * e + DH])
                last.then_inc(s_vbd, 1)

            def step(t, k, it):
                X, Y, Z, E = streams(t)
                y, z, e = t - 1, t - 2, t - 3
                if E:
                    hidden_split(e, 5)
                if Z:
                    lo_parts("x2", z)
                if Y:
                    shift(y, 0)
                if X:
                    norm_stats(0, "ln1", t)
                if Y:
                    shift(y, 1)
                if E:
                    finish(e, (k - 3) % SLOTS)
                if X:
                    normalise(0, "ln1", t)
                if Z:
                    hidden_split(z, 0)
                    hidden_split(z, 1)
                if Y:
                    shift(y, 2)
                    shift(y, 3)
                    sums(y, 0)
                if X:
                    lo_parts("x1", t)
                if Y:
                    sums(y, 1)
                    sums(y, 2)
                    sums(y, 3)
                if Z:
                    hidden_split(z, 2)
                if Y:
                    lo_parts("o", y)
                if Z:
                    hidden_split(z, 3)
                if X:
                    v_blocks(t, 0)
                    v_blocks(t, 1)
                if Y:
                    norm_stats(1, "ln2", y)
                    normalise(1, "ln2", y)
                if Z:
                    hidden_split(z, 4)

            steps(dve, step)

        @block.gpsimd
        def _(pool):
            nc.gpsimd.memset(ident[:, :], 0.0).then_inc(s_id, 1)
            nc.gpsimd.memset(half[:, :], -0.5).then_inc(s_ve[0], 1)
            nc.gpsimd.memset(eps[:, :], EPS).then_inc(s_ve[0], 1)
            pool.wait_ge(s_id, 1)
            nc.gpsimd.affine_select(out=ident[:, :], in_=ident[:, :], compare_op=ALU.not_equal, fill=1.0,
                                    base=0, pattern=[[-1, 128]], channel_multiplier=1).then_inc(s_id, 1)
            pool.wait_ge(s_ve[0], 2)

            def rstd(ln, s):
                pool.wait_ge(s_mv[ln], nth(s, PAIRS, PAIRS - 1))
                n = max(CHUNKS[ln])
                nc.gpsimd.tensor_tensor(ve[ln][0:n, :], mv[ln][0:n, :, 1], eps[0:n, :], ALU.add).then_inc(s_ve[ln], 1)
                pool.wait_ge(s_ve[ln], nth(s, 1, 0) + (2 if ln == 0 else 0))
                nc.gpsimd.tensor_tensor(rs[ln][0:n, :], ve[ln][0:n, :], half[0:n, 0:PAIRS], ALU.pow).then_inc(s_rs[ln], 1)

            def residual(v, k):
                pool.wait_ge(s_yr, nth(v, 1, 0))
                nc.gpsimd.tensor_tensor(xt[0:CR, k, 1, :], yr[:, :], xt[0:CR, k, 1, :], ALU.add).then_inc(s_or, 1)

            def step(t, k, it):
                X, Y, Z, E = streams(t)
                y, e = t - 1, t - 3
                if X:
                    rstd(0, t)
                if E:
                    residual(e, (k - 3) % SLOTS)
                if Y:
                    for j in range(PAIRS):
                        pool.wait_ge(s_rec, nth(y, PAIRS, j))
                        each = rc[:, j, :].unsqueeze(2).to_broadcast([SP, HEADS, N])
                        nc.gpsimd.tensor_tensor(probs(j), probs(j), each, ALU.mult).then_inc(s_prob, 1)
                    rstd(1, y)

            steps(pool, step)


def kernel(x, L0_conv_norm1_w, L0_conv_norm1_b, L0_conv_qkv_w, L0_conv_qkv_b, L0_conv_proj_w, L0_conv_proj_b,
           L0_conv_norm2_w, L0_conv_norm2_b, L0_conv_fc1_w, L0_conv_fc1_b, L0_conv_fc2_w, L0_conv_fc2_b):
    import concourse.bacc as bacc
    from concourse.bass_utils import run_bass_kernel_spmd

    given = {
        "x": x, "norm1_w": L0_conv_norm1_w, "norm1_b": L0_conv_norm1_b,
        "qkv_wt": np.asarray(L0_conv_qkv_w).T, "qkv_b": L0_conv_qkv_b,
        "proj_wt": np.asarray(L0_conv_proj_w).T, "proj_b": L0_conv_proj_b,
        "norm2_w": L0_conv_norm2_w, "norm2_b": L0_conv_norm2_b,
        "fc1_wt": np.asarray(L0_conv_fc1_w).T, "fc1_b": L0_conv_fc1_b,
        "fc2_wt": np.asarray(L0_conv_fc2_w).T, "fc2_b": L0_conv_fc2_b,
    }
    nc = bacc.Bacc("TRN2", target_bir_lowering=False, num_devices=1)
    arrays, args = {}, []
    for name, a in given.items():
        a = np.ascontiguousarray(a)
        arrays[f"in_{name}"] = a
        args.append(nc.dram_tensor(f"in_{name}", a.shape, mybir.dt.from_np(a.dtype), kind="ExternalInput").ap())
    args.append(nc.dram_tensor("out", (B, C, H, W), F32, kind="ExternalOutput").ap())
    swin_block_program(nc, *args)
    return run_bass_kernel_spmd(nc, [arrays], core_ids=[0]).results[0]["out"]
```

```python
import numpy as np
import concourse.bass as bass
from concourse import mybir
from contextlib import ExitStack

F32 = mybir.dt.float32
F32R = mybir.dt.float32r
ALU = mybir.AluOpType
ACT = mybir.ActivationFunctionType
AX = mybir.AxisListType

B, C, H, W = 16, 192, 56, 56
WIN, SHIFT, HEADS = 7, 3, 6
DH = C // HEADS
HID = 4 * C
N = WIN * WIN
NW = W // WIN
NE = N + N % 2
T = NW * N
UPB = H // WIN
UNITS = B * UPB
CM = 128
CR = C - CM
MT = HID // 128
HB = 3
PAIRS = NW // 2
TP = 2 * N
WP = 64
SP = WP + N
ROWS = [2, 2, 2, 1]
CHUNKS = [[W * r for r in ROWS], [TP] * PAIRS]
TM = max(CHUNKS[0])
SLOTS = UPB
AHEAD = SLOTS - 1
SCALE = float(DH) ** -0.5
EPS = 1e-5

PA = 4 * W - SHIFT
PB = T - SHIFT
SMALL = 16 * (12 + 6 + 3 + MT)

BANK_USES = [("x2", 0, 2), ("x2", 1, 3),
             ("s", 0, 0), ("s", 1, 1), ("s", 2, 0), ("s", 3, 1),
             ("pt", 0, 0), ("pt", 1, 1), ("o", 0, 2), ("o", 1, 3), ("pt", 2, 0), ("pt", 3, 1),
             ("vt", 0, 0), ("vt", 1, 1), ("ln2", 0, 2), ("ln2", 1, 3),
             ("x1", 0, 0), ("x1", 1, 1)]
BANK_OF = {(n, i): b for n, i, b in BANK_USES}
LAG = {"x1": 0, "vt": 1, "s": 2, "pt": 2, "o": 2, "ln2": 2, "x2": 3}


def use_before(name, part, t):
    b = BANK_OF[name, part]
    own = [(n, i) for n, i, bank in BANK_USES if bank == b]
    at = own.index((name, part))
    for back in range(1, 4 * len(own)):
        n, i = own[(at - back) % len(own)]
        v = t - (LAG[n] + (back - at + len(own) - 1) // len(own))
        if not isinstance(v, int) or 0 <= v < UNITS:
            return n, i, v
    return None


QKV_COLS = [(2 * C, CM), (2 * C + CM, CR), (0, CM), (C, CM), (CM, CR), (C + CM, CR)]
QKV_TILES = [(0, 128), (128, 64), (192, 128), (320, 128), (448, 128)]


QKV_READS = {4: 3, 3: 7, 2: 8}
QK_COPIES = 8


def nth(unit, per_unit, i):
    return unit * per_unit + (i + 1)


def swin_block_program(nc, x, n1w, n1b, qkv_wt, qkv_b, proj_wt, proj_b, n2w, n2b,
                       fc1_wt, fc1_b, fc2_wt, fc2_b, out):
    ctx = ExitStack()
    with ctx:
        def sb(name, shape, dt=F32):
            return ctx.enter_context(nc.sbuf_tensor(name, shape, dt))

        def sem(name):
            return ctx.enter_context(nc.semaphore(name))

        ident = sb("ident", [128, 128])
        half = sb("half", [128, PAIRS])
        eps = sb("eps", [128, PAIRS])
        NQ, NF = 3 * C, HID
        wq = [sb(f"wq_{p}", [128, NQ], F32R) for p in ("mh", "ml", "rh", "rl")]
        wp = [sb(f"wp_{p}", [128, C], F32R) for p in ("mh", "ml", "rh", "rl")]
        w1 = [sb(f"w1_{p}", [128, NF], F32R) for p in ("mh", "ml", "rh", "rl")]
        w2h = sb("w2h", [128, MT, C], F32R)
        w2l = sb("w2l", [128, MT, CM], F32R)
        w2r = sb("w2r", [128, MT, 128], F32R)
        bq = sb("bq", [128, 5])
        pb = sb("pb", [1, C])
        bp = sb("bp", [64, C], F32R)
        ones = sb("ones", [64, TP], F32R)
        b1 = sb("b1", [128, MT])
        b2 = sb("b2", [128, 2])
        raw_m = sb("raw_m", [128, NF])
        raw_r = sb("raw_r", [128, NF])
        raw_2 = sb("raw_2", [128, MT, C])
        scl_m = sb("scl_m", [128, NF])
        scl_r = sb("scl_r", [128, NF])
        nwb = sb("nwb", [128, 8])

        xt = sb("xt", [128, SLOTS, 2, T])
        st = [sb(f"st{i}", [TM, PAIRS, 6]) for i in range(2)]
        mv = [sb(f"mv{i}", [TM, PAIRS, 2]) for i in range(2)]
        ve = [sb(f"ve{i}", [TM, PAIRS]) for i in range(2)]
        rs = [sb(f"rs{i}", [TM, PAIRS]) for i in range(2)]
        xn = [sb(f"xn{i}", [TM, PAIRS, C]) for i in range(2)]
        x1 = [sb(f"x1_{p}", [128, NW, WP], F32R) for p in ("h", "l", "r")]
        x2 = [sb(f"x2_{p}", [128, T], F32R) for p in ("h", "l", "r")]
        qm = sb("qm", [128, T])
        km = sb("km", [128, NW, 4 * N])
        qr = sb("qr", [CR, T])
        kr = sb("kr", [CR, NW, 2 * N])
        vbd = sb("vbd", [128, NW, 3, WP])
        pr = sb("pr", [SP, PAIRS, HEADS * WP])
        mx = sb("mx", [SP, PAIRS, HEADS])
        sm = sb("sm", [SP, PAIRS, HEADS])
        rc = sb("rc", [SP, PAIRS, HEADS])
        pt = sb("pt", [SP, 2, 3, 128])
        o = [sb(f"o_{p}", [128, T], F32R) for p in ("h", "l", "r")]
        hf = sb("hf", [128, HB, T])
        hh = sb("hh", [128, HB, T], F32R)
        hl = sb("hl", [128, HB, T], F32R)
        yl = sb("yl", [CR, T])
        yr = sb("yr", [CR, T])

        att = ctx.enter_context(nc.psum_tensor("att", [128, 4, 512], F32))
        hid = [ctx.enter_context(nc.psum_tensor(f"hid{i}", [128, 512], F32)) for i in range(2)]
        yps = [ctx.enter_context(nc.psum_tensor(f"yps{i}", [128, 512], F32)) for i in range(2)]

        HI_LO = {"x1": [p[:, :, 0:N] for p in x1]}
        for name, parts in (("x2", x2), ("o", o)):
            HI_LO[name] = [p.rearrange("p (w n) -> p w n", w=NW) for p in parts]

        def bank(name, i):
            if name == "ln1":
                return yps[i][:, :]
            if name == "qkv":
                return hid[i == 3][:, :]
            return att[:, BANK_OF[name, i], :]

        s_raw = [sem(f"raw_loaded_{i}") for i in range(4)]
        s_small = sem("small_loaded")
        s_id = sem("ident_made")
        s_zero = sem("pads_zeroed")
        s_scaled = sem("weights_scaled")
        s_split = sem("weights_split")
        s_rawfree = sem("raw_used_by_bias_products")
        s_bias_mm = sem("bias_products_done")
        s_bias = sem("biases_ready")
        s_x = [sem(f"x_loaded_{i}") for i in range(SLOTS)]
        s_st = [sem(f"out_stored_{i}") for i in range(SLOTS)]
        s_pe = {n: sem(f"pe_{n}") for n in ("ln1", "x1", "qkv", "vt", "s", "pt", "o", "ln2", "x2", "fc1", "fc2")}
        s_stats = [sem(f"bn_stats_done_{i}") for i in range(2)]
        s_seen = sem("bn_stats_seen")
        s_mv = [sem(f"mean_var_done_{i}") for i in range(2)]
        s_ve = [sem(f"var_eps_done_{i}") for i in range(2)]
        s_rs = [sem(f"rstd_done_{i}") for i in range(2)]
        s_norm = [sem(f"normalised_{i}") for i in range(2)]
        s_hi = {n: sem(f"hi_{n}") for n in ("x1", "x2", "o")}
        s_lo = {n: sem(f"lo_{n}") for n in ("x1", "x2", "o")}
        s_qkv = sem("qkv_in_sbuf")
        s_vbd = sem("vbd_ready")
        s_mx = sem("row_max")
        s_sub = sem("max_subtracted")
        s_exp = sem("exp_done")
        s_sum = sem("row_sum")
        s_rec = sem("sum_reciprocal")
        s_prob = sem("probabilities")
        s_ptc = sem("pt_in_sbuf")
        s_gelu = sem("gelu_done")
        s_hh = sem("hidden_hi")
        s_hl = sem("hidden_lo")
        s_hl_last = sem("hidden_lo_last_tile")
        s_ylo = sem("y_rem_lo_copied")
        s_ym = sem("out_main_ready")
        s_yr = sem("y_rem_summed")
        s_or = sem("out_rem_ready")

        xf = x.rearrange("b c h w -> b c (h w)")
        of = out.rearrange("b c h w -> b c (h w)")

        def runs(i):
            a = i * T + SHIFT * W + SHIFT
            b = a + PA
            body = [(a, PB, 0)] if i < UPB - 1 else [(a, PA, 0), (b % (H * W), PB - PA, PA)]
            return body + [(a - SHIFT, SHIFT, PB)]

        def transfers(i):
            return 16 * 2 * len(runs(i))

        def rows_by_window(ap, j):
            r0, n = sum(ROWS[:j]), ROWS[j]
            return ap.rearrange("p (w r c) -> p r w c", r=WIN, w=NW)[:, r0:r0 + n]

        def windows_by_row(ap, j):
            return ap.rearrange("p (r w c) -> p w r c", r=WIN, w=NW)[:, 2 * j:2 * j + 2]

        def last_read(name, i, v):
            if name in ("x1", "x2", "o"):
                return s_lo[name], v, 2, i
            if name == "ln2":
                return s_norm[1], v, PAIRS, 2 * i + 1
            return {"vt": (s_vbd, v, 2, i), "s": (s_sub, v, PAIRS, i), "pt": (s_ptc, v, PAIRS, i)}[name]

        def probs(j):
            return pr[:, j, :].rearrange("p (h m) -> p h m", h=HEADS)[:, :, 0:N]

        def by_window(ps):
            return ps.rearrange("p (w n) -> p w n", w=NW)

        def even(ps):
            return ps[:, 0:NW * NE].rearrange("p (w n) -> p w n", w=NW)

        def five(ps, w, c0, m, act):
            wmh, wml, wrh, wrl = w
            xh, xl, xrr = act
            nc.tensor.matmul(ps, wmh[:, c0:c0 + m], xh, start=True, stop=False)
            nc.tensor.matmul(ps, wml[:, c0:c0 + m], xh, start=False, stop=False)
            nc.tensor.matmul(ps, wmh[:, c0:c0 + m], xl, start=False, stop=False)
            nc.tensor.matmul(ps, wrh[:, c0:c0 + m], xrr, start=False, stop=False)
            return nc.tensor.matmul(ps, wrl[:, c0:c0 + m], xrr, start=False, stop=True)

        def five_tokens(ps, w, act, stop):
            wmh, wml, wrh, wrl = w
            xh, xl, xrr = act
            nc.tensor.matmul(ps, xh, wmh[:, 0:C], start=True, stop=False)
            nc.tensor.matmul(ps, xh, wml[:, 0:C], start=False, stop=False)
            nc.tensor.matmul(ps, xl, wmh[:, 0:C], start=False, stop=False)
            nc.tensor.matmul(ps, xrr, wrh[:, 0:C], start=False, stop=False)
            return nc.tensor.matmul(ps, xrr, wrl[:, 0:C], start=False, stop=stop)

        block = ctx.enter_context(nc.Block())

        @block.sync
        def _(sp):
            def load(b, i):
                if not (isinstance(b, int) and b == 0):
                    sp.wait_ge(s_st[i], b * transfers(i))
                for px, n, at in runs(i):
                    sp.dma_start(xt[:, i, 0, at:at + n], xf[b, 0:CM, px:px + n]).then_inc(s_x[i], 16)
                    sp.dma_start(xt[0:CR, i, 1, at:at + n], xf[b, CM:C, px:px + n]).then_inc(s_x[i], 16)

            def store(b, i):
                sp.wait_ge(s_ym, b * UPB + (i + 1))
                sp.wait_ge(s_or, b * UPB + (i + 1))
                for px, n, at in runs(i):
                    sp.dma_start(of[b, 0:CM, px:px + n], xt[:, i, 0, at:at + n]).then_inc(s_st[i], 16)
                    sp.dma_start(of[b, CM:C, px:px + n], xt[0:CR, i, 1, at:at + n]).then_inc(s_st[i], 16)

            for k, (vec, cols) in enumerate(((n1w, 0), (n1b, 2), (n2w, 4), (n2b, 6))):
                sp.dma_start(nwb[:, cols:cols + 1], vec[0:CM].rearrange("(p a) -> p a", a=1)).then_inc(s_small, 16)
                for h in range(2):
                    sp.dma_start(nwb[h * CR:(h + 1) * CR, cols + 1:cols + 2],
                                 vec[CM:C].rearrange("(p a) -> p a", a=1)).then_inc(s_small, 16)
            at = 0
            for c0, m in QKV_COLS:
                t, r = next((k, at - s) for k, (s, n) in enumerate(QKV_TILES) if s <= at < s + n)
                sp.dma_start(bq[r:r + m, t:t + 1], qkv_b[c0:c0 + m].rearrange("(p a) -> p a", a=1)).then_inc(s_small, 16)
                at += m
            sp.dma_start(b2[:, 0:1], fc2_b[0:CM].rearrange("(p a) -> p a", a=1)).then_inc(s_small, 16)
            sp.dma_start(b2[0:CR, 1:2], fc2_b[CM:C].rearrange("(p a) -> p a", a=1)).then_inc(s_small, 16)
            sp.dma_start(pb[:, :], proj_b.rearrange("(a c) -> a c", a=1)).then_inc(s_small, 16)
            for m in range(MT):
                sp.dma_start(b1[:, m:m + 1], fc1_b[m * 128:(m + 1) * 128].rearrange("(p a) -> p a", a=1)).then_inc(s_small, 16)
            at = 0
            for c0, m in QKV_COLS:
                sp.dma_start(raw_m[:, at:at + m], qkv_wt[0:CM, c0:c0 + m]).then_inc(s_raw[0], 16)
                for h in range(2):
                    sp.dma_start(raw_r[h * CR:(h + 1) * CR, at:at + m], qkv_wt[CM:C, c0:c0 + m]).then_inc(s_raw[0], 16)
                at += m
            sp.dma_start(raw_2[:, :, :], fc2_wt.rearrange("(m p) n -> p m n", p=128)).then_inc(s_raw[3], 16)
            for n, (wt, cols) in enumerate(((proj_wt, C), (fc1_wt, NF))):
                sp.wait_ge(s_rawfree, n + 1)
                sp.dma_start(raw_m[:, 0:cols], wt[0:CM, :]).then_inc(s_raw[n + 1], 16)
                for h in range(2):
                    sp.dma_start(raw_r[h * CR:(h + 1) * CR, 0:cols], wt[CM:C, :]).then_inc(s_raw[n + 1], 16)

            def image(b, following=True):
                for i in range(UPB):
                    store(b, i)
                    if i + AHEAD < UPB:
                        load(b, i + AHEAD)
                    elif following:
                        load(b + 1, i + AHEAD - UPB)

            for i in range(AHEAD):
                load(0, i)
            image(0)
            with sp.Fori(1, B - 1) as b:
                image(b)
            image(B - 1, following=False)
            for i in range(SLOTS):
                sp.wait_ge(s_st[i], B * transfers(i))

        def steps(eng, step):
            for t in range(SLOTS):
                step(t, t, 0)
            with eng.Fori(1, UNITS // SLOTS) as it:
                for k in range(SLOTS):
                    step(it * SLOTS + k, k, it)
            for t in range(UNITS, UNITS + 4):
                step(t, t % SLOTS, t // SLOTS)

        def streams(t):
            return [not isinstance(t, int) or 0 <= t - lag < UNITS for lag in range(5)] + [t - lag for lag in range(1, 5)]

        @block.tensor
        def _(pe):
            pe.wait_ge(s_id, 2)
            pe.wait_ge(s_small, SMALL)

            def claim(name, parts, t):
                waits = []
                for i in parts:
                    use = use_before(name, i, t)
                    if use is not None:
                        done, v, per, n = last_read(*use)
                        if waits and waits[-1][0] is done:
                            n = max(n, waits.pop()[3])
                        waits.append((done, v, per, n))
                for done, v, per, n in waits:
                    pe.wait_ge(done, nth(v, per, n))

            pe.wait_ge(s_raw[0], 16 * 18)
            for t, (c0, m) in enumerate(QKV_TILES):
                nc.tensor.matmul(hid[0][0:m, t:t + 1], raw_m[:, c0:c0 + m], nwb[:, 2:3], start=True, stop=False)
                last = nc.tensor.matmul(hid[0][0:m, t:t + 1], raw_r[0:CR, c0:c0 + m], nwb[0:CR, 3:4], start=False, stop=True)
            last.then_inc(s_bias_mm, 1)
            pe.wait_ge(s_raw[2], 16 * 3)
            for m in range(MT):
                nc.tensor.matmul(hid[1][:, m:m + 1], raw_m[:, m * 128:(m + 1) * 128], nwb[:, 6:7], start=True, stop=False)
                last = nc.tensor.matmul(hid[1][:, m:m + 1], raw_r[0:CR, m * 128:(m + 1) * 128], nwb[0:CR, 7:8], start=False, stop=True)
            last.then_inc(s_bias_mm, 1)
            pe.wait_ge(s_zero, 1)
            pe.wait_ge(s_split, 4)
            pe.wait_ge(s_bias, 2)

            def to_tokens(tile_m, tile_r):
                for j, n in enumerate(CHUNKS[0]):
                    c, cc = j // 2, j % 2
                    at = sum(CHUNKS[0][:j])
                    ps = bank("ln1", c)[0:n, cc * C:(cc + 1) * C]
                    nc.tensor.transpose(ps[:, 0:CM], tile_m[:, at:at + n], ident[:, :])
                    last = nc.tensor.transpose(ps[:, CM:C], tile_r[:, at:at + n], ident[0:CR, 0:CR])
                    if cc == 1:
                        last.then_inc(s_pe["ln1"], 1)

            def project(t):
                for j in range(PAIRS):
                    c, cc = j // 2, j % 2
                    if cc == 0:
                        claim("ln2", (c,), t)
                    ps = bank("ln2", c)[0:TP, cc * C:(cc + 1) * C]
                    five_tokens(ps, wp, [p[:, TP * j:TP * j + TP] for p in o], False)
                    last = nc.tensor.matmul(ps, ones[:, :], bp[:, :], start=False, stop=True)
                    if cc == 1:
                        last.then_inc(s_pe["ln2"], 1)

            def to_channels(name, ln, t, v, place):
                claim(name, (0, 1), t)
                for g, (c0, m) in enumerate(((0, CM), (CM, CR))):
                    for j, n in enumerate(CHUNKS[ln]):
                        if g == 0 and j < 3 and name == "x1":
                            pe.wait_ge(s_norm[ln], nth(v, PAIRS, j + (j == 2)))
                        last = nc.tensor.transpose(place(bank(name, g)[0:m, 0:T], j), xn[ln][0:n, j, c0:c0 + m], ident[0:n, 0:n])
                    last.then_inc(s_pe[name], 1)

            def fc1(t, v, m):
                if m == 0:
                    pe.wait_ge(s_lo["x2"], nth(v, 2, 1))
                    if not isinstance(t, int) or t - 1 < UNITS:
                        pe.wait_ge(s_qkv, nth(t - 1, QK_COPIES, QK_COPIES - 1))
                if m >= 2 or (isinstance(t, int) and t - 1 >= UNITS):
                    pe.wait_ge(s_gelu, v * MT + (m - 1))
                five(hid[m % 2][:, 0:T], w1, m * 128, 128, [p[:, :] for p in x2]).then_inc(s_pe["fc1"], 1)

            def fc2(t, v, m):
                pe.wait_ge(s_hh, nth(v, MT, m))
                if m == 0 and (not isinstance(t, int) or t < UNITS):
                    pe.wait_ge(s_norm[0], nth(t, PAIRS, PAIRS - 1))
                elif m == 0:
                    pe.wait_ge(s_yr, v)
                a, z = m == 0, m == MT - 1
                b = m % HB
                ym, yx = yps[0][:, 0:T], yps[1][:, 0:T]
                nc.tensor.matmul(ym, w2h[:, m, 0:CM], hh[:, b, :], start=a, stop=False)
                nc.tensor.matmul(ym, w2l[:, m, :], hh[:, b, :], start=False, stop=False)
                nc.tensor.matmul(yx, w2r[:, m, :], hh[:, b, :], start=a, stop=z, skip_group_check=True)
                if m < MT - 1:
                    pe.wait_ge(s_hl, nth(v, MT - 1, m))
                else:
                    pe.wait_ge(s_hl_last, nth(v, 1, 0))
                nc.tensor.matmul(ym, w2h[:, m, 0:CM], hl[:, b, :], start=False, stop=z)
                nc.tensor.matmul(yx[0:CR], w2h[:, m, CM:C], hl[:, b, :], start=False, stop=z,
                                 skip_group_check=True).then_inc(s_pe["fc2"], 1)

            def scores(t, v, j):
                claim("s", (j,), t)
                for wi in range(2):
                    w = 2 * j + wi
                    rows = bank("s", j)[WP * wi:WP * wi + N, :]
                    nc.tensor.matmul(rows[:, 0:4 * N], qm[:, N * w:N * w + N], km[:, w, :], start=True, stop=True)
                    last = nc.tensor.matmul(rows[:, 4 * N:6 * N], qr[:, N * w:N * w + N], kr[:, w, :], start=True, stop=True)
                last.then_inc(s_pe["s"], 1)

            def probs_t(t, v, j):
                claim("pt", (j,), t)
                pe.wait_ge(s_prob, nth(v, PAIRS, j))
                for p in range(3):
                    last = nc.tensor.transpose(bank("pt", j)[0:SP, 128 * p:128 * p + SP],
                                               pr[:, j, 2 * WP * p:2 * WP * p + SP], ident[0:SP, 0:SP])
                last.then_inc(s_pe["pt"], 1)

            def weighted(t, v, j):
                if j == 0:
                    pe.wait_ge(s_vbd, nth(v, 2, 1))
                    claim("o", (0, 1), t)
                pe.wait_ge(s_ptc, nth(v, PAIRS, j))
                for wi in range(2):
                    w = 2 * j + wi
                    for p in range(3):
                        ps = bank("o", p // 2)[WP * (p % 2):WP * (p % 2) + WP, N * w:N * w + N]
                        last = nc.tensor.matmul(ps, vbd[0:SP, w, p, :], pt[:, j % 2, p, WP * wi:WP * wi + N],
                                                start=True, stop=True)
                if j == PAIRS - 1:
                    last.then_inc(s_pe["o"], 1)

            def qkv(t, tile):
                c0, m = QKV_TILES[tile]
                if tile == 4 and (not isinstance(t, int) or t >= 4):
                    pe.wait_ge(s_gelu, nth(t - 4, MT, MT - 1))
                elif tile == 2:
                    pe.wait_ge(s_qkv, nth(t - 1, QK_COPIES, QKV_READS[4] - 1))
                five(even(bank("qkv", tile)[0:m]), wq, c0, m, [p[:, :, 0:NE] for p in x1]).then_inc(s_pe["qkv"], 1)

            def values(t):
                for j in range(PAIRS):
                    c, cc = j // 2, j % 2
                    if cc == 0:
                        claim("vt", (c,), t)
                    pairs = [p[:, 2 * j:2 * j + 2, :].rearrange("p w n -> p (w n)") for p in x1]
                    last = five_tokens(bank("vt", c)[:, cc * C:(cc + 1) * C], wq, pairs, True)
                    if cc == 1:
                        last.then_inc(s_pe["vt"], 1)

            def step(t, k, it):
                W_, X, Y, Z, E, x, y, z, e = streams(t)
                if E:
                    fc2(t, e, 3)
                if Z:
                    to_channels("x2", 1, t, z, windows_by_row)
                if Y:
                    pe.wait_ge(s_qkv, nth(y, QK_COPIES, QK_COPIES - 1))
                    scores(t, y, 0)
                    scores(t, y, 1)
                if E:
                    fc2(t, e, 4)
                if Y:
                    scores(t, y, 2)
                    scores(t, y, 3)
                if X:
                    pe.wait_ge(s_lo["x1"], nth(x, 2, 1))
                    qkv(t, 4)
                    qkv(t, 3)
                if E:
                    fc2(t, e, 5)
                if Y:
                    probs_t(t, y, 0)
                    probs_t(t, y, 1)
                if X:
                    qkv(t, 2)
                if Y:
                    weighted(t, y, 0)
                    probs_t(t, y, 2)
                    weighted(t, y, 1)
                    probs_t(t, y, 3)
                if W_:
                    pe.wait_ge(s_x[k], (it + 1) * transfers(k))
                    if E:
                        pe.wait_ge(s_yr, nth(e, 1, 0))
                    to_tokens(xt[:, k, 0, :], xt[0:CR, k, 1, :])
                if Y:
                    weighted(t, y, 2)
                    weighted(t, y, 3)
                if X:
                    values(t)
                if Z:
                    fc1(t, z, 0)
                    fc1(t, z, 1)
                if Y:
                    pe.wait_ge(s_lo["o"], nth(y, 2, 1))
                    project(t)
                if Z:
                    fc2(t, z, 0)
                    fc1(t, z, 2)
                    fc2(t, z, 1)
                    fc1(t, z, 3)
                if W_:
                    to_channels("x1", 0, t, t, rows_by_window)
                if Z:
                    fc2(t, z, 2)
                    fc1(t, z, 4)
                    fc1(t, z, 5)

            steps(pe, step)

        @block.scalar
        def _(act):
            act.wait_ge(s_zero, 1)
            act.wait_ge(s_bias, 2)

            def copy(dst, src, done):
                nc.scalar.activation(dst, src, ACT.Copy).then_inc(done, 1)

            def biased(dst, src, bias, done):
                return nc.scalar.activation(dst, src, ACT.Identity, bias=bias).then_inc(done, 1)

            def hi_parts(name, v, signals):
                for i, (dst, m) in enumerate(((0, CM), (2, CR))):
                    if i < signals:
                        act.wait_ge(s_pe[name], nth(v, signals, i))
                    src = by_window(bank(name, i)[0:m, 0:T])
                    if name == "o":
                        biased(HI_LO[name][dst][0:m], src, bq[0:m, i:i + 1], s_hi[name])
                    else:
                        copy(HI_LO[name][dst][0:m], src, s_hi[name])

            def gelu(v, m):
                act.wait_ge(s_pe["fc1"], nth(v, MT, m))
                for dst, done in ((hh, s_hh), (hf, s_gelu)):
                    nc.scalar.activation(dst[:, m % HB, :], hid[m % 2][:, 0:T], ACT.Gelu, bias=b1[:, m:m + 1]).then_inc(done, 1)

            def y_low(v):
                act.wait_ge(s_pe["fc2"], nth(v, MT, MT - 1))
                copy(yl[:, :], yps[1][CR:128, 0:T], s_ylo)

            def exps(v, j):
                act.wait_ge(s_sub, nth(v, PAIRS, j))
                nc.scalar.activation(probs(j), probs(j), ACT.Exp, scale=SCALE).then_inc(s_exp, 1)

            def pt_copy(v, j):
                act.wait_ge(s_pe["pt"], nth(v, PAIRS, j))
                src = bank("pt", j)[0:SP, 0:384].rearrange("p (a m) -> p a m", a=3)[:, :, 0:SP]
                copy(pt[:, j % 2, :, 0:SP], src, s_ptc)

            by_head = km.rearrange("p w (h n) -> p w h n", h=4)
            by_head_r = kr.rearrange("p w (h n) -> p w h n", h=2)
            places = {2: [(qm.rearrange("p (w n) -> p w n", w=NW), 0, CM)],
                      3: [(by_head[DH * h:DH * h + DH, :, h, :], DH * h, DH) for h in range(4)],
                      4: [(qr.rearrange("p (w n) -> p w n", w=NW), 0, CR)]
                         + [(by_head_r[DH * h:DH * h + DH, :, h, :], CR + DH * h, DH) for h in range(2)]}

            def qkv_out(v, i, tile):
                act.wait_ge(s_pe["qkv"], nth(v, 3, i))
                for dst, r, m in places[tile]:
                    biased(dst, even(bank("qkv", tile)[r:r + m])[:, :, 0:N], bq[r:r + m, tile:tile + 1], s_qkv)

            def step(t, k, it):
                W_, X, Y, Z, E, x, y, z, e = streams(t)
                if Z:
                    hi_parts("x2", z, 2)
                if Y:
                    exps(y, 0)
                    exps(y, 1)
                if Y:
                    exps(y, 2)
                if X:
                    qkv_out(x, 0, 4)
                if Y:
                    exps(y, 3)
                    pt_copy(y, 0)
                    pt_copy(y, 1)
                if E:
                    y_low(e)
                if X:
                    qkv_out(x, 1, 3)
                if Y:
                    pt_copy(y, 2)
                    pt_copy(y, 3)
                if X:
                    qkv_out(x, 2, 2)
                if Y:
                    hi_parts("o", y, 1)
                if Z:
                    gelu(z, 0)
                    gelu(z, 1)
                if Z:
                    gelu(z, 2)
                    gelu(z, 3)
                if W_:
                    hi_parts("x1", t, 2)
                if Z:
                    gelu(z, 4)
                    gelu(z, 5)

            steps(act, step)

        @block.vector
        def _(dve):
            for t in (*x1, bp):
                nc.vector.memset(t[:].bitcast(F32), 0.0)
            for t in (km, kr, vbd, pr, pt, mv[0], mv[1]):
                nc.vector.memset(t[:], 0.0)
            nc.vector.memset(ones[:, :].bitcast(F32), 1.0)
            nc.vector.memset(att[:, :, :], 0.0).then_inc(s_zero, 1)

            scaled = 1
            dve.wait_ge(s_small, SMALL)
            dve.wait_ge(s_zero, 1)
            nc.vector.tensor_copy(bp[0:1, :], pb[:, :]).then_inc(s_scaled, 1)
            dve.wait_ge(s_scaled, scaled)
            nc.vector.tensor_tensor(bp[32:33, :], pb[:, :], bp[0:1, :].bitcast(F32), ALU.subtract)
            for n, (w, cols, nw) in enumerate(((wq, NQ, 0), (wp, C, None), (w1, NF, 4))):
                dve.wait_ge(s_raw[n], 16 * (18 if n == 0 else 3))
                sm_, sr_ = raw_m, raw_r
                if nw is not None:
                    if n:
                        dve.wait_ge(s_split, n)
                    nc.vector.tensor_scalar(scl_m[:, 0:cols], raw_m[:, 0:cols], nwb[:, nw:nw + 1], None, ALU.mult).then_inc(s_scaled, 1)
                    nc.vector.tensor_scalar(scl_r[:, 0:cols], raw_r[:, 0:cols], nwb[:, nw + 1:nw + 2], None, ALU.mult).then_inc(s_scaled, 1)
                    scaled += 2
                    dve.wait_ge(s_scaled, scaled)
                    sm_, sr_ = scl_m, scl_r
                nc.vector.tensor_copy(w[0][:, :], sm_[:, 0:cols]).then_inc(s_scaled, 1)
                nc.vector.tensor_copy(w[2][:, :], sr_[:, 0:cols]).then_inc(s_scaled, 1)
                scaled += 2
                dve.wait_ge(s_scaled, scaled)
                nc.vector.tensor_tensor(w[1][:, :], sm_[:, 0:cols], w[0][:, :].bitcast(F32), ALU.subtract)
                nc.vector.tensor_tensor(w[3][:, :], sr_[:, 0:cols], w[2][:, :].bitcast(F32), ALU.subtract).then_inc(s_split, 1)
                if n < 2:
                    if n == 0:
                        dve.wait_ge(s_bias_mm, 1)
                    dve.wait_ge(s_split, n + 1)
                    dve.sem_inc(s_rawfree, 1)
            dve.wait_ge(s_raw[3], 16)
            nc.vector.tensor_copy(w2h[:, :, :], raw_2[:, :, :]).then_inc(s_scaled, 1)
            nc.vector.tensor_copy(w2r[:, :, 0:CR], raw_2[:, :, CM:C]).then_inc(s_scaled, 1)
            dve.wait_ge(s_scaled, scaled + 2)
            nc.vector.tensor_tensor(w2l[:, :, :], raw_2[:, :, 0:CM], w2h[:, :, 0:CM].bitcast(F32), ALU.subtract)
            nc.vector.tensor_tensor(w2r[:, :, CR:128], raw_2[:, :, CM:C], w2r[:, :, 0:CR].bitcast(F32), ALU.subtract).then_inc(s_split, 1)
            dve.wait_ge(s_bias_mm, 1)
            for t, (c0, m) in enumerate(QKV_TILES):
                last = nc.vector.tensor_tensor(bq[0:m, t:t + 1], bq[0:m, t:t + 1], hid[0][0:m, t:t + 1], ALU.add)
            last.then_inc(s_bias, 1)
            dve.wait_ge(s_bias_mm, 2)
            nc.vector.tensor_tensor(b1[:, :], b1[:, :], hid[1][:, 0:MT], ALU.add).then_inc(s_bias, 1)

            def norm_stats(ln, name, s):
                for j, n in enumerate(CHUNKS[ln]):
                    c, cc = j // 2, j % 2
                    if cc == 0:
                        dve.wait_ge(s_pe[name], nth(s, 2, c))
                    nc.vector.bn_stats(st[ln][0:n, j, :], bank(name, c)[0:n, cc * C:(cc + 1) * C]).then_inc(s_stats[ln], 1)
                dve.wait_ge(s_stats[ln], nth(s, PAIRS, PAIRS - 1))
                dve.sem_inc(s_seen, 1)
                for j, n in enumerate(CHUNKS[ln]):
                    nc.vector.bn_aggr(mv[ln][0:n, j, :], st[ln][0:n, j, :]).then_inc(s_mv[ln], 1)

            def normalise(ln, name, s, first, end):
                dve.wait_ge(s_rs[ln], nth(s, 1, 0))
                for j in range(first, end):
                    n = CHUNKS[ln][j]
                    c, cc = j // 2, j % 2
                    nc.vector.tensor_scalar(xn[ln][0:n, j, :], bank(name, c)[0:n, cc * C:(cc + 1) * C], mv[ln][0:n, j, 0:1],
                                            rs[ln][0:n, j:j + 1], ALU.subtract, ALU.mult).then_inc(s_norm[ln], 1)

            def lo_parts(name, v):
                xh, xl, xrr = HI_LO[name]
                dve.wait_ge(s_hi[name], nth(v, 2, 0))
                for i, (lo, m, hi) in enumerate(((xl, CM, xh), (xrr[CR:128], CR, xrr[0:CR]))):
                    if i:
                        dve.wait_ge(s_hi[name], nth(v, 2, 1))
                    src = by_window(bank(name, i)[0:m, 0:T])
                    if name == "o":
                        nc.vector.scalar_tensor_tensor(out=lo, in0=src, scalar=bq[0:m, i:i + 1], in1=hi.bitcast(F32),
                                                       op0=ALU.add, op1=ALU.subtract).then_inc(s_lo[name], 1)
                    else:
                        nc.vector.tensor_tensor(lo, src, hi.bitcast(F32), ALU.subtract).then_inc(s_lo[name], 1)

            def hidden_lo(v, m):
                dve.wait_ge(s_gelu, nth(v, MT, m))
                b = m % HB
                nc.vector.tensor_tensor(hl[:, b, :], hf[:, b, :], hh[:, b, :].bitcast(F32), ALU.subtract).then_inc(s_hl, 1)

            def finish(v, k):
                dve.wait_ge(s_pe["fc2"], nth(v, MT, MT - 1))
                nc.vector.scalar_tensor_tensor(out=xt[:, k, 0, :], in0=yps[0][:, 0:T], scalar=b2[:, 0:1],
                                               in1=xt[:, k, 0, :], op0=ALU.add, op1=ALU.add).then_inc(s_ym, 1)
                dve.wait_ge(s_ylo, nth(v, 1, 0))
                if not (isinstance(v, int) and v == 0):
                    dve.wait_ge(s_or, v)
                nc.vector.scalar_tensor_tensor(out=yr[:, :], in0=yps[1][0:CR, 0:T], scalar=b2[0:CR, 1:2],
                                               in1=yl[:, :], op0=ALU.add, op1=ALU.add).then_inc(s_yr, 1)

            def shift(v, j):
                dve.wait_ge(s_pe["s"], nth(v, PAIRS, j))
                sc = bank("s", j)[0:SP, 0:HEADS * N].rearrange("p (h m) -> p h m", m=N)
                nc.vector.reduce_max(mx[:, j, :], sc, AX.X).then_inc(s_mx, 1)
                dve.wait_ge(s_mx, nth(v, PAIRS, j))
                most = mx[:, j, :].unsqueeze(2).to_broadcast([SP, HEADS, N])
                nc.vector.tensor_tensor(probs(j), sc, most, ALU.subtract).then_inc(s_sub, 1)

            def sums(v, j):
                dve.wait_ge(s_exp, nth(v, PAIRS, j))
                nc.vector.reduce_sum(sm[:, j, :], probs(j), AX.X).then_inc(s_sum, 1)
                dve.wait_ge(s_sum, nth(v, PAIRS, j))
                nc.vector.reciprocal(rc[:, j, :], sm[:, j, :]).then_inc(s_rec, 1)

            def v_blocks(s, c):
                dve.wait_ge(s_pe["vt"], nth(s, 2, c))
                src = bank("vt", c)[:, 0:2 * C].rearrange("p (j a d) -> p j a d", j=2, a=3)
                dst = vbd[:, 4 * c:4 * c + 4, :, :].rearrange("p (j w) a d -> p w j a d", w=2)
                for wi in range(2):
                    for e in range(2):
                        last = nc.vector.tensor_copy(dst[WP * e:WP * e + WP, wi, :, :, DH * e:DH * e + DH],
                                                     src[WP * wi:WP * wi + WP, :, :, DH * e:DH * e + DH])
                last.then_inc(s_vbd, 1)

            def step(t, k, it):
                W_, X, Y, Z, E, x, y, z, e = streams(t)
                if Z:
                    lo_parts("x2", z)
                if Y:
                    shift(y, 0)
                    shift(y, 1)
                    sums(y, 0)
                    shift(y, 2)
                    sums(y, 1)
                    shift(y, 3)
                    sums(y, 2)
                    sums(y, 3)
                if E:
                    finish(e, (k - 4) % SLOTS)
                if W_:
                    norm_stats(0, "ln1", t)
                if X:
                    v_blocks(x, 0)
                if Y:
                    lo_parts("o", y)
                if W_:
                    normalise(0, "ln1", t, 0, PAIRS)
                if X:
                    v_blocks(x, 1)
                if Z:
                    hidden_lo(z, 0)
                    hidden_lo(z, 1)
                if Y:
                    norm_stats(1, "ln2", y)
                if Z:
                    hidden_lo(z, 2)
                if Y:
                    normalise(1, "ln2", y, 0, 2)
                if Z:
                    hidden_lo(z, 3)
                if Y:
                    normalise(1, "ln2", y, 2, PAIRS)
                if W_:
                    lo_parts("x1", t)
                if Z:
                    hidden_lo(z, 4)

            steps(dve, step)

        @block.gpsimd
        def _(pool):
            nc.gpsimd.memset(ident[:, :], 0.0).then_inc(s_id, 1)
            nc.gpsimd.memset(half[:, :], -0.5).then_inc(s_ve[0], 1)
            nc.gpsimd.memset(eps[:, :], EPS).then_inc(s_ve[0], 1)
            pool.wait_ge(s_id, 1)
            nc.gpsimd.affine_select(out=ident[:, :], in_=ident[:, :], compare_op=ALU.not_equal, fill=1.0,
                                    base=0, pattern=[[-1, 128]], channel_multiplier=1).then_inc(s_id, 1)
            pool.wait_ge(s_ve[0], 2)

            def rstd(ln, s):
                pool.wait_ge(s_mv[ln], nth(s, PAIRS, PAIRS - 1))
                n = max(CHUNKS[ln])
                nc.gpsimd.tensor_tensor(ve[ln][0:n, :], mv[ln][0:n, :, 1], eps[0:n, :], ALU.add).then_inc(s_ve[ln], 1)
                pool.wait_ge(s_ve[ln], nth(s, 1, 0) + (2 if ln == 0 else 0))
                nc.gpsimd.tensor_tensor(rs[ln][0:n, :], ve[ln][0:n, :], half[0:n, 0:PAIRS], ALU.pow).then_inc(s_rs[ln], 1)

            def hidden_lo_last(v):
                pool.wait_ge(s_gelu, nth(v, MT, MT - 1))
                b = (MT - 1) % HB
                nc.gpsimd.tensor_tensor(hl[:, b, :], hf[:, b, :], hh[:, b, :].bitcast(F32), ALU.subtract).then_inc(s_hl_last, 1)

            def residual(v, k):
                pool.wait_ge(s_yr, nth(v, 1, 0))
                nc.gpsimd.tensor_tensor(xt[0:CR, k, 1, :], yr[:, :], xt[0:CR, k, 1, :], ALU.add).then_inc(s_or, 1)

            def step(t, k, it):
                W_, X, Y, Z, E, x, y, z, e = streams(t)
                if E:
                    hidden_lo_last(e)
                if Y:
                    for j in range(PAIRS):
                        pool.wait_ge(s_rec, nth(y, PAIRS, j))
                        each = rc[:, j, :].unsqueeze(2).to_broadcast([SP, HEADS, N])
                        nc.gpsimd.tensor_tensor(probs(j), probs(j), each, ALU.mult).then_inc(s_prob, 1)
                if E:
                    residual(e, (k - 4) % SLOTS)
                if W_:
                    rstd(0, t)
                if Y:
                    rstd(1, y)

            steps(pool, step)


def kernel(x, L0_conv_norm1_w, L0_conv_norm1_b, L0_conv_qkv_w, L0_conv_qkv_b, L0_conv_proj_w, L0_conv_proj_b,
           L0_conv_norm2_w, L0_conv_norm2_b, L0_conv_fc1_w, L0_conv_fc1_b, L0_conv_fc2_w, L0_conv_fc2_b):
    import concourse.bacc as bacc
    from concourse.bass_utils import run_bass_kernel_spmd

    given = {
        "x": x, "norm1_w": L0_conv_norm1_w, "norm1_b": L0_conv_norm1_b,
        "qkv_wt": np.asarray(L0_conv_qkv_w).T, "qkv_b": L0_conv_qkv_b,
        "proj_wt": np.asarray(L0_conv_proj_w).T, "proj_b": L0_conv_proj_b,
        "norm2_w": L0_conv_norm2_w, "norm2_b": L0_conv_norm2_b,
        "fc1_wt": np.asarray(L0_conv_fc1_w).T, "fc1_b": L0_conv_fc1_b,
        "fc2_wt": np.asarray(L0_conv_fc2_w).T, "fc2_b": L0_conv_fc2_b,
    }
    nc = bacc.Bacc("TRN2", target_bir_lowering=False, num_devices=1)
    arrays, args = {}, []
    for name, a in given.items():
        a = np.ascontiguousarray(a)
        arrays[f"in_{name}"] = a
        args.append(nc.dram_tensor(f"in_{name}", a.shape, mybir.dt.from_np(a.dtype), kind="ExternalInput").ap())
    args.append(nc.dram_tensor("out", (B, C, H, W), F32, kind="ExternalOutput").ap())
    swin_block_program(nc, *args)
    return run_bass_kernel_spmd(nc, [arrays], core_ids=[0]).results[0]["out"]
```
